# Optimizing a Trainium2 kernel written in Bass

```python
import numpy as np
import jax
import jax.numpy as jnp

def _softmax(x, axis=-1):
    return jax.nn.softmax(x, axis=axis)

def _gelu(x):
    return jax.nn.gelu(x, approximate=True)

def _silu(x):
    return jax.nn.silu(x)

def _sigmoid(x):
    return jax.nn.sigmoid(x)

def _layernorm(x, axis=-1, eps=1e-05):
    m = jnp.mean(x, axis=axis, keepdims=True)
    v = jnp.var(x, axis=axis, keepdims=True)
    return (x - m) / jnp.sqrt(v + eps)

def _scatter_add(tgt, idx, src, axis=0):
    return tgt.at[idx].add(src)

def _segment_sum(src, seg, n):
    return jax.ops.segment_sum(src, seg, n)
kernel_name = 'mk_adaln_ffn_d1_seqx_r2_9d275b'

def setup_inputs(seed: int=0):
    np.random.seed(seed)
    _w = jnp.asarray

    def _rec_inputs():
        import jax
        import jax.numpy as jnp
        _rk = jax.random.key(seed)
        x = -0.0002928 + 1 * jax.random.normal(jax.random.fold_in(_rk, 1), (16, 512, 512), jnp.float32)
        _lenS = 512 - jax.random.randint(jax.random.fold_in(_rk, 7), (16,), 0, max(1, 512 // 4) + 1, jnp.int32)
        _lenS2 = 512 - jax.random.randint(jax.random.fold_in(_rk, 8), (16,), 0, max(1, 512 // 4) + 1, jnp.int32)
        fside_16xSxS_0 = -5.72187e-05 + 0.999849 * jax.random.normal(jax.random.fold_in(_rk, 11), (16, 512, 512), jnp.float32)
        cond_64 = -0.0265395 + 0.99382 * jax.random.normal(jax.random.fold_in(_rk, 13), (16, 64), jnp.float32)
        _validS = jnp.arange(512)[None, :] < _lenS[:, None]
        _validS2 = jnp.arange(512)[None, :] < _lenS2[:, None]
        _causal = jnp.tril(jnp.ones((512, 512), dtype=bool))
        mask_BxS_bk0 = jnp.logical_not(jnp.broadcast_to(_validS[:, :], (16, 512)))
        return (x, fside_16xSxS_0, cond_64, mask_BxS_bk0)
    x, fside_16xSxS_0, cond_64, mask_BxS_bk0 = _rec_inputs()

    def _L0_cond_setup():
        import jax, jax.numpy as jnp
        import numpy as np
        B, N, DIM, H, DH = (2, 1024, 512, 16, 64)
        INNER = H * DH
        EPS = 1e-05

        def layernorm(x, g):
            mean = jnp.mean(x, axis=-1, keepdims=True)
            var = jnp.var(x, axis=-1, keepdims=True)
            return (x - mean) * jax.lax.rsqrt(var + EPS) * g
        key = jax.random.key(seed)
        ks = jax.random.split(key, 10)
        x = jax.random.normal(ks[0], (B, N, DIM), dtype=jnp.float32)
        attn_bias = jax.random.normal(ks[1], (H, N, N), dtype=jnp.float32)
        mask = jax.random.randint(ks[2], (B, N), 0, 2).astype(bool)
        g_in = jnp.ones((DIM,), dtype=jnp.float32)
        null_attn_bias = jax.random.normal(ks[3], (H,), dtype=jnp.float32)
        null_kv = jax.random.normal(ks[4], (2, DH), dtype=jnp.float32)
        Wq = jax.random.normal(ks[5], (DIM, INNER), dtype=jnp.float32) * 0.02
        Wkv = jax.random.normal(ks[6], (DIM, 2 * DH), dtype=jnp.float32) * 0.02
        Wo = jax.random.normal(ks[7], (INNER, DIM), dtype=jnp.float32) * 0.02
        g_out = jnp.ones((DIM,), dtype=jnp.float32)
        return {'x': x, 'attn_bias': attn_bias, 'mask': mask, 'g_in': g_in, 'null_attn_bias': null_attn_bias, 'null_kv': null_kv, 'Wq': Wq, 'Wkv': Wkv, 'Wo': Wo, 'g_out': g_out}
    _L0_cond_all = _L0_cond_setup()
    _L0_cond_in = {k: v for k, v in _L0_cond_all.items() if k in ('g_in', 'null_attn_bias', 'Wq', 'Wkv', 'Wo', 'g_out')}
    del _L0_cond_all

    def _L0_ffn_setup():
        import jax, jax.numpy as jnp
        import numpy as np
        import math
        B, L, D = (4, 2048, 512)
        F = 2048
        E = 16
        CAP_FACTOR = 1.0
        EPS = 1e-05
        key = jax.random.key(seed)
        ks = jax.random.split(key, 8)
        std = 0.02
        return {'x': jax.random.normal(ks[0], (B, L, D), dtype=jnp.float32), 'norm_weight': jnp.ones((D,), dtype=jnp.float32), 'router_weight': jax.random.normal(ks[1], (E, D), dtype=jnp.float32) * std, 'router_bias': jnp.zeros((E,), dtype=jnp.float32), 'fc1_weight': jax.random.normal(ks[2], (E, F, D), dtype=jnp.float32) * std, 'fc1_bias': jnp.zeros((E, F), dtype=jnp.float32), 'fc2_weight': jax.random.normal(ks[3], (E, D, F), dtype=jnp.float32) * std, 'fc2_bias': jnp.zeros((E, D), dtype=jnp.float32)}
    _L0_ffn_all = _L0_ffn_setup()
    _L0_ffn_in = {k: v for k, v in _L0_ffn_all.items() if k in ('norm_weight', 'router_weight', 'router_bias', 'fc1_weight', 'fc1_bias', 'fc2_weight', 'fc2_bias')}
    del _L0_ffn_all
    return {'x': x, 'fside_16xSxS_0': fside_16xSxS_0, 'cond_64': cond_64, 'mask_BxS_bk0': mask_BxS_bk0, 'L0_cond_g_in': _L0_cond_in['g_in'], 'L0_cond_null_attn_bias': _L0_cond_in['null_attn_bias'], 'L0_cond_Wq': _L0_cond_in['Wq'], 'L0_cond_Wkv': _L0_cond_in['Wkv'], 'L0_cond_Wo': _L0_cond_in['Wo'], 'L0_cond_g_out': _L0_cond_in['g_out'], 'L0_ffn_norm_weight': _L0_ffn_in['norm_weight'], 'L0_ffn_router_weight': _L0_ffn_in['router_weight'], 'L0_ffn_router_bias': _L0_ffn_in['router_bias'], 'L0_ffn_fc1_weight': _L0_ffn_in['fc1_weight'], 'L0_ffn_fc1_bias': _L0_ffn_in['fc1_bias'], 'L0_ffn_fc2_weight': _L0_ffn_in['fc2_weight'], 'L0_ffn_fc2_bias': _L0_ffn_in['fc2_bias']}

def reference(x, fside_16xSxS_0, cond_64, mask_BxS_bk0, L0_cond_g_in, L0_cond_null_attn_bias, L0_cond_Wq, L0_cond_Wkv, L0_cond_Wo, L0_cond_g_out, L0_ffn_norm_weight, L0_ffn_router_weight, L0_ffn_router_bias, L0_ffn_fc1_weight, L0_ffn_fc1_bias, L0_ffn_fc2_weight, L0_ffn_fc2_bias):
    import jax
    import jax.numpy as jnp

    def _L0_cond_ref(x, attn_bias, mask, g_in, null_attn_bias, null_kv, Wq, Wkv, Wo, g_out):
        import jax, jax.numpy as jnp
        import numpy as np
        B, N, DIM, H, DH = (2, 1024, 512, 16, 64)
        INNER = H * DH
        EPS = 1e-05

        def layernorm(x, g):
            mean = jnp.mean(x, axis=-1, keepdims=True)
            var = jnp.var(x, axis=-1, keepdims=True)
            return (x - mean) * jax.lax.rsqrt(var + EPS) * g
        b, n, _ = x.shape
        scale = DH ** (-0.5)
        xn = layernorm(x, g_in)
        q = (xn @ Wq).reshape(b, n, H, DH).transpose(0, 2, 1, 3) * scale
        kv = xn @ Wkv
        k, v = (kv[..., :DH], kv[..., DH:])
        nk = jnp.broadcast_to(null_kv[0], (b, 1, DH))
        nv = jnp.broadcast_to(null_kv[1], (b, 1, DH))
        k = jnp.concatenate([nk, k], axis=1)
        v = jnp.concatenate([nv, v], axis=1)
        sim = jnp.einsum('bhid,bjd->bhij', q, k)
        null_col = jnp.broadcast_to(null_attn_bias[:, None, None], (H, n, 1))
        bias = jnp.concatenate([null_col, attn_bias], axis=-1)
        sim = sim + bias
        neg = -jnp.finfo(sim.dtype).max
        j = n + 1
        causal_mask = jnp.triu(jnp.ones((n, j), dtype=bool), k=j - n + 1)
        sim = jnp.where(causal_mask, neg, sim)
        mask_p = jnp.pad(mask, ((0, 0), (1, 0)), constant_values=True)
        sim = jnp.where(mask_p[:, None, None, :], sim, neg)
        attn = jax.nn.softmax(sim, axis=-1)
        out = jnp.einsum('bhij,bjd->bhid', attn, v)
        out = out.transpose(0, 2, 1, 3).reshape(b, n, INNER)
        out = out @ Wo
        return layernorm(out, g_out)

    def _L0_ffn_ref(x, norm_weight, router_weight, router_bias, fc1_weight, fc1_bias, fc2_weight, fc2_bias):
        import jax, jax.numpy as jnp
        import numpy as np
        import math
        B, L, D = (4, 2048, 512)
        F = 2048
        E = 16
        CAP_FACTOR = 1.0
        EPS = 1e-05
        b, l, d = x.shape
        n_tokens = b * l
        n_experts = router_weight.shape[0]
        capacity = max(1, math.ceil(CAP_FACTOR * n_tokens / n_experts))
        top_k = min(capacity, n_tokens)
        xf = x.reshape(n_tokens, d)
        rms = jnp.sqrt(jnp.mean(xf * xf, axis=-1, keepdims=True) + EPS)
        xn = xf / rms * norm_weight
        logits = xn @ router_weight.T + router_bias
        probs = jax.nn.softmax(logits, axis=-1)
        _, idx = jax.lax.top_k(logits.T, top_k)
        xe = xn[idx]
        h = jnp.einsum('ecd,efd->ecf', xe, fc1_weight) + fc1_bias[:, None, :]
        h = jax.nn.gelu(h, approximate=False)
        y = jnp.einsum('ecf,edf->ecd', h, fc2_weight) + fc2_bias[:, None, :]
        gates = jnp.take_along_axis(probs.T, idx, axis=1)
        flat_idx = idx.reshape(-1)
        contrib = (y * gates[:, :, None]).reshape(-1, d)
        output = jnp.zeros((n_tokens, d), dtype=x.dtype).at[flat_idx].add(contrib)
        gate_sums = jnp.zeros((n_tokens, 1), dtype=x.dtype).at[flat_idx].add(gates.reshape(-1, 1))
        assigned = gate_sums > 0
        output = jnp.where(assigned, output / jnp.where(assigned, gate_sums, 1.0), output)
        return output.reshape(b, l, d)
    x = x + _L0_ffn_ref(_L0_cond_ref(x, fside_16xSxS_0, mask_BxS_bk0, L0_cond_g_in, L0_cond_null_attn_bias, cond_64, L0_cond_Wq, L0_cond_Wkv, L0_cond_Wo, L0_cond_g_out), L0_ffn_norm_weight, L0_ffn_router_weight, L0_ffn_router_bias, L0_ffn_fc1_weight, L0_ffn_fc1_bias, L0_ffn_fc2_weight, L0_ffn_fc2_bias)
    return x

_drawn_inputs = setup_inputs


def setup_inputs(seed=0):
    import zlib

    import numpy as np

    out = dict(_drawn_inputs(seed))
    spreads = {'L0_cond_g_in': (1.0, 0.6),
     'L0_cond_g_out': (1.0, 0.54),
     'L0_ffn_norm_weight': (1.0, 0.6),
     'L0_ffn_router_bias': (0.0, 0.8),
     'L0_ffn_fc1_bias': (0.0, 0.677),
     'L0_ffn_fc2_bias': (0.0, 0.363)}
    factors = {}
    for name, (base, spread) in spreads.items():
        noise = np.random.default_rng([zlib.crc32(name.encode()), seed]).standard_normal(out[name].shape)
        drawn = base * np.exp(spread * noise) if base else spread * noise
        out[name] = jnp.asarray(drawn.astype(out[name].dtype))
    for name, factor in factors.items():
        out[name] = (out[name] * factor).astype(out[name].dtype)
    return out
```

```python
from contextlib import ExitStack

import concourse.bass as bass
import concourse.mybir as mybir
from concourse.alu_op_type import AluOpType as ALU

F32 = mybir.dt.float32
F32R = mybir.dt.float32r
BF16 = mybir.dt.bfloat16
I32 = mybir.dt.int32
U32 = mybir.dt.uint32
U8 = mybir.dt.uint8
ACT = mybir.ActivationFunctionType
AX_X = mybir.AxisListType.X

P = 128
B, S, D = 16, 512, 512
H, DH = 16, 64
E, F = 16, 2048
N = B * S
NT = N // P
QT = S // P
KD = D // P
KO = H * DH // P
CAP = N // E
CT = CAP // P
FT = F // P
GH = 4
NG = H // GH
VW = DH + 2
SCALE = DH ** -0.5
EPS = 1e-5
MASKED = -1e30
NONE = NT
QCOLS, KCOLS = 5, 4
NPAIR = 256
EP = E + 2
META = 32


class Count:

    def __init__(self, eng, sem, base=0):
        self.eng, self.sem, self.base, self.n = eng, sem, base, 0

    def inc(self, instruction):
        instruction.then_inc(self.sem, 1)
        self.n += 1

    def wait(self):
        self.eng.wait_ge(self.sem, self.base + self.n)

    def step(self, instruction):
        self.inc(instruction)
        self.wait()


def f32(ap):
    return ap.bitcast(F32)


def spread(ap, shape):
    return ap.unsqueeze(len(ap.shape)).to_broadcast(shape)


def alone(eng, passed):
    eng.sem_inc(passed, 1)


def make_lists(nc, ctx, io, keep):
    with ExitStack() as scope:
        def sb(name, shape, dt=F32):
            return scope.enter_context(nc.sbuf_tensor("lists_" + name, shape, dt))

        def sem(name):
            return ctx.enter_context(nc.semaphore("lists_" + name))

        mask8 = sb("mask8", [P, N], U8)
        wq_raw = sb("wq_raw", [P, KD, H * DH])
        wo_raw = sb("wo_raw", [P, KO, D])
        wkv_raw = sb("wkv_raw", [P, KD, 3 * DH])
        nk_raw = sb("nk_raw", [P, 2])
        seen = sb("seen", [P, NT])
        seen_pair = sb("seen_pair", [P, NT, QT])
        tri = sb("tri", [P, QT, QT])
        zero = sb("zero", [P, NT * QT])
        rank_q = sb("rank_q", [P, NT])
        rank_k = sb("rank_k", [P, NT * QT])
        slot = sb("slot", [P, 2])
        first = sb("first", [P, 1])
        tile_id = sb("tile_id", [P, NT])
        key_tile = sb("key_tile", [P, NT * QT])
        bias_tile = sb("bias_tile", [P, NT * QT])
        off_diag = sb("off_diag", [P, NT * QT])
        diag = sb("diag", [P, NT * QT])
        begin = sb("begin", [P, NT])
        end = sb("end", [P, NT])
        hit_q = sb("hit_q", [P, NT])
        hit_k = sb("hit_k", [P, 2, NT * QT])
        junk = sb("junk", [P, NT * QT])
        ql = sb("ql", [P, QCOLS])
        kl = sb("kl", [P, 2, KCOLS])
        ql_i = sb("ql_i", [P, QCOLS], I32)
        kl_i = sb("kl_i", [P, 2, KCOLS], I32)

        mask_in, raw_in = sem("mask_in"), sem("raw_in")
        const_in = sem("const_in")
        iotas_done, slots_done, ident_done = sem("iotas_done"), sem("slots_done"), sem("ident_done")
        hi_done, hidden_done = sem("hi_done"), sem("hidden_done")
        setup_step, lists_done, lists_out, lists_in = (
            sem("setup_step"), sem("lists_done"), sem("lists_out"), sem("lists_in"))
        copied = keep["x_copied"]
        splits = ((wkv_raw, keep["wkv_hi"], keep["wkv_lo"]), (wq_raw, keep["wq_hi"], keep["wq_lo"]),
                  (wo_raw, keep["wo_hi"], keep["wo_lo"]), (nk_raw, keep["nk_hi"], keep["nk_lo"]))

        with nc.Block() as block:
            @block.sync
            def _(sp):
                sp.dma_start(mask8[:, :], io["mask"].to_broadcast([P, N])).then_inc(mask_in, 16)
                sp.dma_start(wkv_raw[:, :, :], io["wkv"]).then_inc(raw_in, 16)
                sp.dma_start(wq_raw[:, :, :], io["wq"]).then_inc(raw_in, 16)
                sp.dma_start(wo_raw[:, :, :], io["wo"]).then_inc(raw_in, 16)
                sp.dma_start(nk_raw[:, :], io["nk"]).then_inc(raw_in, 16)
                for name in ("g_in", "g_out", "norm_w"):
                    sp.dma_start(keep[name][:, :], io[name].to_broadcast([P, D])).then_inc(const_in, 16)
                sp.dma_start(keep["null_bias"][:, :], io["null_bias"].to_broadcast([P, H])).then_inc(const_in, 16)
                sp.dma_start(keep["router_b"][:, :], io["router_b"].to_broadcast([P, E])).then_inc(const_in, 16)
                sp.dma_start(keep["null_v"][:, :], io["null_v"].to_broadcast([P, VW])).then_inc(const_in, 16)
                sp.dma_start(keep["router_wT"][:, :, :], io["router_wT"]).then_inc(const_in, 16)
                sp.dma_start(io["out"].rearrange("(a n) d -> a (n d)", a=16),
                             io["x"].rearrange("(a n) d -> a (n d)", a=16)).then_inc(copied, 16)
                sp.wait_ge(const_in, 7 * 16)
                sp.dma_start(keep["xn_dram"][0:N, :].rearrange("(t p) d -> p t d", p=P),
                             keep["g_in"][:, :].unsqueeze(1).to_broadcast([P, NT, D])).then_inc(keep["xn_filled"], 16)
                sp.wait_ge(lists_done, 1)
                sp.dma_start(keep["ql_dram"][:, :], ql_i[:, :]).then_inc(lists_out, 16)
                sp.dma_start(keep["kl_dram"].rearrange("(a p) c -> p a c", p=P), kl_i[:, :, :]).then_inc(lists_out, 16)
                sp.wait_ge(lists_out, 32)
                sp.dma_start(keep["ql"][:, :], keep["ql_dram"].rearrange("(o p) c -> o (p c)", o=1)).then_inc(lists_in, 16)
                sp.dma_start(keep["kl"][:, :], keep["kl_dram"].rearrange("(o p) c -> o (p c)", o=1)).then_inc(lists_in, 16)
                sp.wait_ge(lists_in, 32)

            @block.gpsimd
            def _(pool):
                ident = keep["ident"]
                pool.iota(slot[:, :], [[P, 2]], base=0, channel_multiplier=1,
                          allow_small_or_imprecise_dtypes=True).then_inc(slots_done, 1)
                pool.iota(tile_id[:, :], [[1, NT]], base=0, channel_multiplier=0,
                          allow_small_or_imprecise_dtypes=True).then_inc(iotas_done, 1)
                pool.iota(key_tile[:, :], [[QT, B], [0, QT], [1, QT]], base=0, channel_multiplier=0,
                          allow_small_or_imprecise_dtypes=True).then_inc(iotas_done, 1)
                pool.iota(bias_tile[:, :], [[0, B], [QT, QT], [1, QT]], base=0, channel_multiplier=0,
                          allow_small_or_imprecise_dtypes=True).then_inc(iotas_done, 1)
                pool.iota(off_diag[:, :], [[0, B], [1, QT], [-1, QT]], base=0, channel_multiplier=0,
                          allow_small_or_imprecise_dtypes=True).then_inc(iotas_done, 1)
                pool.memset(ident[:, :], 0.0).then_inc(ident_done, 1)
                pool.memset(keep["causal"][:, :, :], 0.0).then_inc(ident_done, 1)
                pool.memset(keep["half"][:, :], -0.5).then_inc(ident_done, 1)
                pool.wait_ge(ident_done, 3)
                pool.affine_select(out=ident[:, :], in_=ident[:, :], compare_op=ALU.not_equal, fill=1.0,
                                   base=0, pattern=[[-1, P]], channel_multiplier=1).then_inc(ident_done, 1)
                pool.affine_select(out=keep["causal"][:, 1, :], in_=keep["causal"][:, 1, :],
                                   compare_op=ALU.is_ge, fill=MASKED, base=0, pattern=[[-1, P]],
                                   channel_multiplier=1).then_inc(ident_done, 1)
                pool.wait_ge(ident_done, 5)

            @block.scalar
            def _(act):
                act.wait_ge(mask_in, 16)
                nc.scalar.activation(keep["hidden"][:, 0:NT, :], mask8[:, :].rearrange("p (t j) -> p t j", j=P),
                                     ACT.Copy, bias=MASKED, scale=-MASKED).then_inc(hidden_done, 1)
                act.wait_ge(raw_in, 64)
                for raw, hi, _ in splits:
                    nc.scalar.activation(hi[:], raw[:], ACT.Copy).then_inc(hi_done, 1)
                act.wait_ge(hidden_done, 1)

            @block.vector
            def _(dve):
                step = Count(dve, setup_step)
                dve.wait_ge(const_in, 7 * 16)
                step.inc(nc.vector.tensor_scalar(keep["null_bias"][:, :], keep["null_bias"][:, :], -1.0, None, ALU.mult))
                step.inc(nc.vector.memset(keep["hidden"][:, NT, :], MASKED))
                step.inc(nc.vector.memset(keep["logits"][:, :, :], 0.0))
                step.inc(nc.vector.memset(zero[:, :], 0.0))
                step.inc(nc.vector.memset(keep["v_hi"][:, DH:DH + 1].bitcast(F32), 1.0))
                step.inc(nc.vector.memset(keep["v_hi"][:, DH + 1:VW].bitcast(F32), 0.0))
                step.inc(nc.vector.memset(keep["v_lo"][:, DH:VW].bitcast(F32), 0.0))
                step.step(nc.vector.memset(tri[:, :, :], 1.0))
                for q in range(QT - 1):
                    step.inc(nc.vector.memset(tri[:, q, q + 1:QT], 0.0))
                has = keep["has_key"]
                seen4 = seen[:, :].rearrange("p (b q) -> p b q", q=QT)
                has4 = has[:, :].rearrange("p (b q) -> p b q", q=QT)
                dve.wait_ge(mask_in, 16)
                step.step(nc.vector.tensor_reduce(has[:, :], mask8[:, :].rearrange("p (t j) -> p t j", j=P), AX_X, ALU.max))
                step.step(nc.vector.tensor_copy(seen4[:, :, 0], has4[:, :, 0]))
                for q in range(1, QT):
                    step.step(nc.vector.tensor_tensor(seen4[:, :, q], seen4[:, :, q - 1], has4[:, :, q], ALU.max))
                pair5 = seen_pair[:, :, :].rearrange("p (b q) k -> p b q k", q=QT)
                for q in range(QT):
                    step.step(nc.vector.tensor_tensor(pair5[:, :, q, :], has4,
                                                      tri[:, q, :].unsqueeze(1).to_broadcast([P, B, QT]), ALU.mult))
                pairs = seen_pair[:, :, :].rearrange("p t k -> p (t k)")
                step.inc(nc.vector.tensor_tensor_scan(rank_q[:, :], seen[:, :], zero[:, 0:NT], 0.0, ALU.add, ALU.add))
                step.inc(nc.vector.tensor_copy(keep["seen"][:, :], seen[:, :]))
                step.step(nc.vector.tensor_tensor_scan(rank_k[:, :], pairs, zero[:, :], 0.0, ALU.add, ALU.add))
                last = rank_k[:, :].rearrange("p (t k) -> p t k", k=QT)[:, :, QT - 1]
                step.inc(nc.vector.tensor_scalar(end[:, :], last, 1.0, None, ALU.add))
                step.step(nc.vector.tensor_reduce(begin[:, :], seen_pair[:, :, :], AX_X, ALU.add))
                dve.wait_ge(iotas_done, 4)
                dve.wait_ge(slots_done, 1)
                step.inc(nc.vector.tensor_tensor(begin[:, :], end[:, :], begin[:, :], ALU.subtract))
                step.inc(nc.vector.tensor_scalar(first[:, :], slot[:, 0:1], 0.0, None, ALU.is_equal))
                step.inc(nc.vector.tensor_scalar(diag[:, :], off_diag[:, :], 0.0, None, ALU.is_equal))
                step.step(nc.vector.scalar_tensor_tensor(hit_q[:, :], rank_q[:, :], slot[:, 0:1], seen[:, :],
                                                         ALU.is_equal, ALU.mult))
                for a in range(2):
                    step.step(nc.vector.scalar_tensor_tensor(hit_k[:, a, :], rank_k[:, :], slot[:, a:a + 1], pairs,
                                                             ALU.is_equal, ALU.mult))
                for c, column in ((0, tile_id), (1, tile_id), (2, begin), (3, end)):
                    step.step(nc.vector.scalar_tensor_tensor(junk[:, 0:NT], hit_q[:, :], 1.0, column[:, :], ALU.mult,
                                                             ALU.mult, accum_out=ql[:, c:c + 1]))
                for a in range(2):
                    for c, column in ((0, key_tile), (1, key_tile), (2, bias_tile), (3, diag)):
                        step.step(nc.vector.scalar_tensor_tensor(junk[:, :], hit_k[:, a, :], 1.0, column[:, :],
                                                                 ALU.mult, ALU.mult, accum_out=kl[:, a, c:c + 1]))
                step.inc(nc.vector.scalar_tensor_tensor(ql[:, 0:1], first[:, :], float(NONE), ql[:, 0:1], ALU.mult, ALU.add))
                step.inc(nc.vector.tensor_tensor(ql[:, 3:4], ql[:, 3:4], first[:, :], ALU.add))
                step.inc(nc.vector.scalar_tensor_tensor(kl[:, 0, 1:2], first[:, :], float(NONE), kl[:, 0, 1:2],
                                                        ALU.mult, ALU.add))
                step.step(nc.vector.tensor_scalar(ql[:, 4:5], rank_q[:, NT - 1:NT], 1.0, None, ALU.add))
                step.inc(nc.vector.tensor_copy(kl_i[:, :, :], kl[:, :, :]))
                step.step(nc.vector.tensor_copy(ql_i[:, :], ql[:, :]))
                nc.vector.memset(junk[:, 0:1], 0.0).then_inc(lists_done, 1)
                for n, (raw, hi, lo) in enumerate(splits):
                    dve.wait_ge(hi_done, n + 1)
                    step.inc(nc.vector.tensor_tensor(lo[:], raw[:], f32(hi[:]), ALU.subtract))
                step.wait()


def matmul3(nc, out, left, right, first, last):
    (lh, ll), (rh, rl) = left, right
    nc.tensor.matmul(out, lh, rh, start=first, stop=False)
    nc.tensor.matmul(out, lh, rl, start=False, stop=False)
    return nc.tensor.matmul(out, ll, rh, start=False, stop=last)


def attend(nc, ctx, io, keep):
    with ExitStack() as scope:
        def sb(name, shape, dt=F32):
            return scope.enter_context(nc.sbuf_tensor("attend_" + name, shape, dt))

        def sem(name):
            return ctx.enter_context(nc.semaphore("attend_" + name))

        def bank(name):
            return scope.enter_context(nc.psum_tensor("attend_" + name, [P, 512], F32))

        k_x = sb("k_x", [P, D])
        k_n = sb("k_n", [P, D])
        kx_hi = sb("kx_hi", [P, KD, P], F32R)
        kx_lo = sb("kx_lo", [P, KD, P], F32R)
        kT_hi = sb("kT_hi", [P, P], F32R)
        kT_lo = sb("kT_lo", [P, P], F32R)
        q_x = sb("q_x", [P, D])
        q_n = sb("q_n", [P, D])
        qx_hi = sb("qx_hi", [P, KD, P], F32R)
        qx_lo = sb("qx_lo", [P, KD, P], F32R)
        qT_hi = sb("qT_hi", [P, KO, P], F32R)
        qT_lo = sb("qT_lo", [P, KO, P], F32R)
        bias_raw = sb("bias_raw", [P, H, P])
        bias = sb("bias", [P, H, P])
        hide = sb("hide", [P, P])
        sc = sb("sc", [P, H, P])
        pT_hi = sb("pT_hi", [P, H, P], F32R)
        pT_lo = sb("pT_lo", [P, H, P], F32R)
        neg_max = sb("neg_max", [P, H])
        neg_new = sb("neg_new", [P, H])
        neg_tile = sb("neg_tile", [P, H])
        drop = sb("drop", [P, H])
        alpha = sb("alpha", [P, H])
        acc = sb("acc", [P, H, VW])
        inv_sum = sb("inv_sum", [P, H])
        o = sb("o", [P, H, DH])
        oT_hi = sb("oT_hi", [P, KO, P], F32R)
        oT_lo = sb("oT_lo", [P, KO, P], F32R)
        y = sb("y", [P, D])
        y_sq = sb("y_sq", [P, D])
        xn = sb("xn", [P, D])
        xnT = sb("xnT", [P, KD, P])
        k_st, k_mv, k_r = sb("k_st", [P, 6]), sb("k_mv", [P, 2]), sb("k_r", [P, 1])
        q_st, q_mv, q_r = sb("q_st", [P, 6]), sb("q_mv", [P, 2]), sb("q_r", [P, 1])
        o_st, o_mv, o_r = sb("o_st", [P, 6]), sb("o_mv", [P, 2]), sb("o_r", [P, 1])
        y_ms, y_r = sb("y_ms", [P, 1]), sb("y_r", [P, 1])

        b_s = [bank("b_s0"), bank("b_s1")]
        b_pT, b_pv, b_kx, b_kv, b_6, b_7 = (bank(n) for n in ("b_pT", "b_pv", "b_kx", "b_kv", "b_6", "b_7"))
        b_qx = b_xnT = b_s[0]
        b_q = [b_s[1], b_pT]
        b_o = b_pv
        b_oT = [b_6, b_7]
        b_null, b_logit = b_7, b_6

        k_in, q_in, bias_in, xn_out = sem("k_in"), sem("q_in"), sem("bias_in"), sem("xn_out")
        k_stats, k_rstd, k_normed, kx_ready, kx_hi_ready, kx_lo_ready = (
            sem(n) for n in ("k_stats", "k_rstd", "k_normed", "kx_ready", "kx_hi_ready", "kx_lo_ready"))
        kv_ready, kT_hi_ready, v_hi_ready, kT_ready, v_ready = (
            sem(n) for n in ("kv_ready", "kT_hi_ready", "v_hi_ready", "kT_ready", "v_ready"))
        bias_ready, scores_ready, scores_biased, max_ready, alpha_ready, probs_ready = (
            sem(n) for n in ("bias_ready", "scores_ready", "scores_biased", "max_ready", "alpha_ready", "probs_ready"))
        pT_ready, pT_hi_ready, pT_lo_ready, pv_ready, acc_ready = (
            sem(n) for n in ("pT_ready", "pT_hi_ready", "pT_lo_ready", "pv_ready", "acc_ready"))
        q_stats, q_rstd, q_normed, qx_ready, qx_hi_ready, qx_lo_ready = (
            sem(n) for n in ("q_stats", "q_rstd", "q_normed", "qx_ready", "qx_hi_ready", "qx_lo_ready"))
        q_ready, qT_hi_ready, qT_ready, null_ready, max_begun, acc_begun = (
            sem(n) for n in ("q_ready", "qT_hi_ready", "qT_ready", "null_ready", "max_begun", "acc_begun"))
        o_ready, oT_ready, oT_hi_ready, oT_lo_ready, proj_ready, o_stats, o_rstd = (
            sem(n) for n in ("o_ready", "oT_ready", "oT_hi_ready", "oT_lo_ready", "proj_ready", "o_stats", "o_rstd"))
        y_ready, y_squared, y_rrms, xn_ready, xnT_ready, xnT_copied, logit_ready, logits_kept = (
            sem(n) for n in ("y_ready", "y_squared", "y_rrms", "xn_ready", "xnT_ready", "xnT_copied",
                             "logit_ready", "logits_kept"))
        v_key, v_pair, v_query, v_out = sem("v_key"), sem("v_pair"), sem("v_query"), sem("v_out")
        g_key, g_hide, g_query, g_out, g_rms = (
            sem("g_key"), sem("g_hide"), sem("g_query"), sem("g_out"), sem("g_rms"))
        passed = sem("passed")
        V_KEY, V_PAIR, V_QUERY, V_OUT = 2, 2 * NG + 1, 2, 3

        ident, half = keep["ident"], keep["half"]

        def number(eng, table, at, most, least=0):
            return eng.value_load(table[0:1, bass.ds(at, 1)], min_val=least, max_val=most)

        def tiles(eng, body_pair, body_tile):
            with eng.Fori(0, number(eng, keep["ql"], 4, NT + 1, 1)) as u:
                begin = number(eng, keep["ql"], u * QCOLS + 2, NPAIR - 2)
                end = number(eng, keep["ql"], u * QCOLS + 3, NPAIR - 2)
                with eng.Fori(begin, end) as p:
                    body_pair(u, p)
                body_tile(u, end)

        with nc.Block() as block:
            @block.sync
            def _(sp):
                def load_key(n):
                    at = number(sp, keep["kl"], n * KCOLS, NT - 1)
                    sp.dma_start(k_x[:, :], io["x"][bass.ds(at * P, P), :]).then_inc(k_in, 16)

                def load_query(n):
                    at = number(sp, keep["ql"], n * QCOLS + 1, NT - 1)
                    sp.dma_start(q_x[:, :], io["x"][bass.ds(at * P, P), :]).then_inc(q_in, 16)

                def load_bias(n):
                    at = number(sp, keep["kl"], n * KCOLS + 2, QT * QT - 1)
                    sp.dma_start(bias_raw[:, :, :], io["bias"][bass.ds(at * P, P), :]
                                 .rearrange("p (h j) -> p h j", h=H)).then_inc(bias_in, 16)

                load_query(0)
                load_key(0)
                load_bias(0)
                sp.wait_ge(q_normed, 1)
                load_query(1)
                sp.wait_ge(k_normed, 1)
                load_key(1)
                sp.wait_ge(bias_ready, NG)
                load_bias(1)

                def pair(u, p):
                    sp.wait_ge(k_normed, p + 2)
                    load_key(p + 2)
                    sp.wait_ge(bias_ready, (p + 2) * NG)
                    load_bias(p + 2)

                sp.wait_ge(keep["xn_filled"], 16)

                def tile(u, end):
                    sp.wait_ge(q_normed, u + 2)
                    load_query(u + 2)
                    at = number(sp, keep["ql"], u * QCOLS, NT)
                    sp.wait_ge(xn_ready, u + 1)
                    sp.dma_start(keep["xn_dram"][bass.ds(at * P, P), :], xn[:, :]).then_inc(xn_out, 16)

                tiles(sp, pair, tile)
                n_tiles = number(sp, keep["ql"], 4, NT + 1, 1)
                last = number(sp, keep["ql"], (n_tiles - 1) * QCOLS + 3, NPAIR - 2)
                sp.wait_ge(xn_out, n_tiles * 16)
                sp.wait_ge(q_in, (n_tiles + 2) * 16)
                sp.wait_ge(k_in, (last + 2) * 16)
                sp.wait_ge(bias_in, (last + 2) * 16)
                alone(sp, passed)

            @block.gpsimd
            def _(pool):
                def root(n, variance, scale, out, ready, steps, done):
                    pool.wait_ge(ready, n + 1)
                    alone(pool, passed)
                    nc.gpsimd.tensor_scalar(out, variance, scale, EPS, ALU.mult, ALU.add).then_inc(steps, 1)
                    pool.wait_ge(steps, n + 1)
                    nc.gpsimd.tensor_tensor(out, out, half[:, :], ALU.pow).then_inc(done, 1)

                def key_root(n):
                    root(n, k_mv[:, 1:2], 1.0, k_r[:, :], k_stats, g_key, k_rstd)

                def query_root(n):
                    root(n, q_mv[:, 1:2], 1.0, q_r[:, :], q_stats, g_query, q_rstd)

                def mask_tile(n):
                    kt = number(pool, keep["kl"], n * KCOLS + 1, NT)
                    dg = number(pool, keep["kl"], n * KCOLS + 3, 1)
                    pool.wait_ge(bias_ready, n * NG)
                    nc.gpsimd.tensor_tensor(hide[:, :], keep["hidden"][:, bass.ds(kt, 1), :].rearrange("p o j -> p (o j)"),
                                            keep["causal"][:, bass.ds(dg, 1), :].rearrange("p o j -> p (o j)"),
                                            ALU.add).then_inc(g_hide, 1)
                    pool.wait_ge(g_hide, n + 1)
                    pool.wait_ge(bias_in, (n + 1) * 16)

                def bias_group(c):
                    g = slice(c * GH, (c + 1) * GH)
                    nc.gpsimd.tensor_tensor(bias[:, g, :], bias_raw[:, g, :],
                                            hide[:, :].unsqueeze(1).to_broadcast([P, GH, P]),
                                            ALU.add).then_inc(bias_ready, 1)

                def begin_acc():
                    alone(pool, passed)
                    nc.gpsimd.tensor_copy(acc[:, :, :], keep["null_v"][:, :].unsqueeze(1).to_broadcast([P, H, VW]))\
                        .then_inc(acc_begun, 1)

                begin_acc()
                query_root(0)
                key_root(0)
                mask_tile(0)
                for c in range(NG):
                    bias_group(c)

                def pair(u, p):
                    mask_tile(p + 1)
                    for c in range(NG):
                        pool.wait_ge(scores_biased, p * NG + c + 1)
                        bias_group(c)
                        if c == 1:
                            key_root(p + 1)

                def tile(u, end):
                    pool.wait_ge(o_ready, u + 1)
                    begin_acc()
                    query_root(u + 1)
                    root(u, o_mv[:, 1:2], 1.0, o_r[:, :], o_stats, g_out, o_rstd)
                    root(u, y_ms[:, :], 1.0 / D, y_r[:, :], y_squared, g_rms, y_rrms)

                tiles(pool, pair, tile)

            @block.scalar
            def _(act):
                def part(out, source, ready, count, done):
                    act.wait_ge(ready, count)
                    nc.scalar.activation(out, source, ACT.Copy).then_inc(done, 1)

                def key_rows(n):
                    part(kx_hi[:, :, :], b_kx[:, :].rearrange("p (k t) -> p k t", k=KD), kx_ready, n + 1, kx_hi_ready)

                def key_parts(n):
                    part(kT_hi[:, :], b_kv[:, 0:P], kv_ready, n + 1, kT_hi_ready)

                def value_parts(n):
                    act.wait_ge(kT_ready, n + 1)
                    part(keep["v_hi"][:, 0:DH], b_kv[:, P:P + DH], kv_ready, n + 1, v_hi_ready)

                def query_parts(n):
                    part(qx_hi[:, :, :], b_qx[:, :].rearrange("p (k t) -> p k t", k=KD), qx_ready, n + 1, qx_hi_ready)
                    for a in range(2):
                        part(qT_hi[:, 4 * a:4 * a + 4, :], b_q[a][:, :].rearrange("p (g t) -> p g t", g=4),
                             q_ready, 2 * n + a + 1, qT_hi_ready)

                query_parts(0)
                key_rows(0)
                key_parts(0)
                value_parts(0)

                def pair(u, p):
                    def probs(c):
                        act.wait_ge(max_ready, p * NG + c + 1)
                        for h in range(c * GH, (c + 1) * GH):
                            last = nc.scalar.activation(sc[:, h, :], sc[:, h, :], ACT.Exp, bias=neg_new[:, h:h + 1])
                        last.then_inc(probs_ready, 1)
                        nc.scalar.activation(alpha[:, c * GH:(c + 1) * GH], drop[:, c * GH:(c + 1) * GH], ACT.Exp)\
                            .then_inc(alpha_ready, 1)

                    def probs_part(c):
                        part(pT_hi[:, c * GH:(c + 1) * GH, :], b_pT[:, :].rearrange("p (h t) -> p h t", h=GH),
                             pT_ready, p * NG + c + 1, pT_hi_ready)

                    probs(0)
                    probs(1)
                    probs_part(0)
                    probs(2)
                    probs_part(1)
                    probs(3)
                    key_rows(p + 1)
                    probs_part(2)
                    probs_part(3)
                    key_parts(p + 1)
                    act.wait_ge(pv_ready, (p + 1) * NG)
                    value_parts(p + 1)

                def tile(u, end):
                    for a in range(2):
                        part(oT_hi[:, 4 * a:4 * a + 4, :], b_oT[a][:, :].rearrange("p (g t) -> p g t", g=4),
                             oT_ready, 2 * u + a + 1, oT_hi_ready)
                    query_parts(u + 1)
                    act.wait_ge(y_ready, u + 1)
                    nc.scalar.activation(y_sq[:, :], y[:, :], ACT.Square, accum_out=y_ms[:, :]).then_inc(y_squared, 1)
                    part(xnT[:, :, :], b_xnT[:, :].rearrange("p (k t) -> p k t", k=KD), xnT_ready, u + 1, xnT_copied)

                tiles(act, pair, tile)

            @block.vector
            def _(dve):
                def rest(out, source, hi, ready, count, done):
                    dve.wait_ge(ready, count)
                    nc.vector.tensor_tensor(out, source, f32(hi), ALU.subtract).then_inc(done, 1)

                def stats(n, source, st, mv, steps, per, done):
                    step = Count(dve, steps, n * per)
                    step.step(nc.vector.bn_stats(st[:, :], source))
                    alone(dve, passed)
                    nc.vector.bn_aggr(mv[:, :], st[:, :]).then_inc(done, 1)
                    return step

                def norm(out, source, mv, r, gain, step, done):
                    step.step(nc.vector.tensor_scalar(out, source, mv[:, 0:1], r[:, :], ALU.subtract, ALU.mult))
                    nc.vector.tensor_tensor(out, out, gain[:, :], ALU.mult).then_inc(done, 1)

                def key_stats(n):
                    dve.wait_ge(k_in, (n + 1) * 16)
                    return stats(n, k_x[:, :], k_st, k_mv, v_key, V_KEY, k_stats)

                def key_norm(n, step):
                    dve.wait_ge(k_rstd, n + 1)
                    norm(k_n[:, :], k_x[:, :], k_mv, k_r, keep["g_in"], step, k_normed)

                def key_rows(n):
                    rest(kx_lo[:, :, :], b_kx[:, :].rearrange("p (k t) -> p k t", k=KD), kx_hi[:, :, :],
                         kx_hi_ready, n + 1, kx_lo_ready)

                def key_parts(n):
                    rest(kT_lo[:, :], b_kv[:, 0:P], kT_hi[:, :], kT_hi_ready, n + 1, kT_ready)

                def value_parts(n):
                    rest(keep["v_lo"][:, 0:DH], b_kv[:, P:P + DH], keep["v_hi"][:, 0:DH], v_hi_ready, n + 1, v_ready)

                def query_stats(n):
                    dve.wait_ge(q_in, (n + 1) * 16)
                    return stats(n, q_x[:, :], q_st, q_mv, v_query, V_QUERY, q_stats)

                def query_norm(n, step):
                    dve.wait_ge(q_rstd, n + 1)
                    norm(q_n[:, :], q_x[:, :], q_mv, q_r, keep["g_in"], step, q_normed)
                    assert step.n == V_QUERY

                def query_rows(n):
                    rest(qx_lo[:, :, :], b_qx[:, :].rearrange("p (k t) -> p k t", k=KD), qx_hi[:, :, :],
                         qx_hi_ready, n + 1, qx_lo_ready)

                def query_parts(n):
                    for a in range(2):
                        rest(qT_lo[:, 4 * a:4 * a + 4, :], b_q[a][:, :].rearrange("p (g t) -> p g t", g=4),
                             qT_hi[:, 4 * a:4 * a + 4, :], qT_hi_ready, 2 * n + a + 1, qT_ready)

                def begin_max(n):
                    dve.wait_ge(null_ready, n + 1)
                    nc.vector.scalar_tensor_tensor(
                        neg_max[:, :].rearrange("p (r g) -> p r g", r=2),
                        b_null[:, 0:H].rearrange("p (g r) -> p r g", r=2), -SCALE,
                        keep["null_bias"][:, :].rearrange("p (r g) -> p r g", r=2),
                        ALU.mult, ALU.add).then_inc(max_begun, 1)

                step = query_stats(0)
                query_norm(0, step)
                query_rows(0)
                step = key_stats(0)
                key_norm(0, step)
                query_parts(0)
                begin_max(0)
                key_rows(0)
                key_parts(0)
                value_parts(0)

                def pair(u, p):
                    step = Count(dve, v_pair, p * V_PAIR)

                    def scores(c):
                        g = slice(c * GH, (c + 1) * GH)
                        dve.wait_ge(bias_ready, p * NG + c + 1)
                        dve.wait_ge(scores_ready, p * NG + c + 1)
                        nc.vector.scalar_tensor_tensor(sc[:, g, :], b_s[c % 2][:, :].rearrange("p (h t) -> p h t", h=GH),
                                                       SCALE, bias[:, g, :], ALU.mult, ALU.add).then_inc(scores_biased, 1)
                        dve.wait_ge(scores_biased, p * NG + c + 1)
                        step.step(nc.vector.tensor_reduce(neg_tile[:, g], sc[:, g, :], AX_X, ALU.max, negate=True))
                        step.step(nc.vector.tensor_tensor(neg_new[:, g], neg_max[:, g], neg_tile[:, g], ALU.min))
                        nc.vector.tensor_tensor(drop[:, g], neg_new[:, g], neg_max[:, g], ALU.subtract)\
                            .then_inc(max_ready, 1)

                    def probs_part(c):
                        g = slice(c * GH, (c + 1) * GH)
                        rest(pT_lo[:, g, :], b_pT[:, :].rearrange("p (h t) -> p h t", h=GH), pT_hi[:, g, :],
                             pT_hi_ready, p * NG + c + 1, pT_lo_ready)

                    def accumulate(c):
                        dve.wait_ge(alpha_ready, p * NG + c + 1)
                        dve.wait_ge(pv_ready, p * NG + c + 1)
                        for n in range(GH):
                            h = c * GH + n
                            last = nc.vector.scalar_tensor_tensor(acc[:, h, :], acc[:, h, :], alpha[:, h:h + 1],
                                                                  b_pv[:, n * VW:(n + 1) * VW], ALU.mult, ALU.add)
                        last.then_inc(acc_ready, 1)

                    dve.wait_ge(max_begun, u + 1)
                    dve.wait_ge(v_pair, p * V_PAIR)
                    scores(0)
                    scores(1)
                    key_step = key_stats(p + 1)
                    scores(2)
                    probs_part(0)
                    scores(3)
                    dve.wait_ge(max_ready, (p + 1) * NG)
                    step.inc(nc.vector.tensor_copy(neg_max[:, :], neg_new[:, :]))
                    key_norm(p + 1, key_step)
                    assert key_step.n == V_KEY
                    dve.wait_ge(acc_begun, u + 1)
                    probs_part(1)
                    accumulate(0)
                    probs_part(2)
                    accumulate(1)
                    key_rows(p + 1)
                    probs_part(3)
                    accumulate(2)
                    key_parts(p + 1)
                    accumulate(3)
                    value_parts(p + 1)
                    assert step.n == V_PAIR

                def tile(u, end):
                    step = Count(dve, v_out, u * V_OUT)
                    dve.wait_ge(acc_ready, end * NG)
                    step.step(nc.vector.reciprocal(inv_sum[:, :], acc[:, :, DH]))
                    nc.vector.tensor_tensor(o[:, :, :], acc[:, :, 0:DH], spread(inv_sum[:, :], [P, H, DH]), ALU.mult)\
                        .then_inc(o_ready, 1)
                    query_step = query_stats(u + 1)
                    for a in range(2):
                        rest(oT_lo[:, 4 * a:4 * a + 4, :], b_oT[a][:, :].rearrange("p (g t) -> p g t", g=4),
                             oT_hi[:, 4 * a:4 * a + 4, :], oT_hi_ready, 2 * u + a + 1, oT_lo_ready)
                    query_norm(u + 1, query_step)
                    query_rows(u + 1)
                    dve.wait_ge(proj_ready, u + 1)
                    step.step(nc.vector.bn_stats(o_st[:, :], b_o[:, :]))
                    alone(dve, passed)
                    nc.vector.bn_aggr(o_mv[:, :], o_st[:, :]).then_inc(o_stats, 1)
                    query_parts(u + 1)
                    begin_max(u + 1)
                    dve.wait_ge(o_rstd, u + 1)
                    norm(y[:, :], b_o[:, :], o_mv, o_r, keep["g_out"], step, y_ready)
                    assert step.n == V_OUT
                    dve.wait_ge(y_rrms, u + 1)
                    dve.wait_ge(xn_out, u * 16)
                    nc.vector.scalar_tensor_tensor(xn[:, :], y[:, :], y_r[:, :], keep["norm_w"][:, :],
                                                   ALU.mult, ALU.mult).then_inc(xn_ready, 1)
                    at = number(dve, keep["ql"], u * QCOLS, NT)
                    dve.wait_ge(logit_ready, u + 1)
                    nc.vector.tensor_tensor(keep["logits"][:, bass.ds(at, 1), :].rearrange("p o e -> p (o e)"),
                                            b_logit[:, 0:E], keep["router_b"][:, :], ALU.add).then_inc(logits_kept, 1)

                tiles(dve, pair, tile)

            @block.tensor
            def _(pe):
                def turn(b, source, n, ready, count, done):
                    pe.wait_ge(ready, count)
                    for k in range(n):
                        last = nc.tensor.transpose(b[:, k * P:(k + 1) * P], source(k), ident[:, :])
                    last.then_inc(done, 1)

                def key_rows(n):
                    turn(b_kx, lambda k: k_n[:, k * P:(k + 1) * P], KD, k_normed, n + 1, kx_ready)

                def keys_values(n):
                    pe.wait_ge(kx_lo_ready, n + 1)
                    hi, lo = keep["wkv_hi"], keep["wkv_lo"]
                    for k in range(KD):
                        matmul3(nc, b_kv[:, 0:P], (hi[:, k, 0:P], lo[:, k, 0:P]), (kx_hi[:, k, :], kx_lo[:, k, :]),
                                k == 0, k == KD - 1)
                    for k in range(KD):
                        last = matmul3(nc, b_kv[:, P:P + DH], (kx_hi[:, k, :], kx_lo[:, k, :]),
                                       (hi[:, k, P:P + DH], lo[:, k, P:P + DH]), k == 0, k == KD - 1)
                    last.then_inc(kv_ready, 1)

                def query_rows(n):
                    turn(b_qx, lambda k: q_n[:, k * P:(k + 1) * P], KD, q_normed, n + 1, qx_ready)

                def queries(n):
                    pe.wait_ge(qx_lo_ready, n + 1)
                    for g in range(KO):
                        cols = slice(g * P, (g + 1) * P)
                        for k in range(KD):
                            last = matmul3(nc, b_q[g // 4][:, (g % 4) * P:(g % 4 + 1) * P],
                                           (keep["wq_hi"][:, k, cols], keep["wq_lo"][:, k, cols]),
                                           (qx_hi[:, k, :], qx_lo[:, k, :]), k == 0, k == KD - 1)
                        if g % 4 == 3:
                            last.then_inc(q_ready, 1)

                def null_scores(n):
                    pe.wait_ge(qT_ready, 2 * n + 2)
                    for g in range(KO):
                        last = matmul3(nc, b_null[:, 2 * g:2 * g + 2], (qT_hi[:, g, :], qT_lo[:, g, :]),
                                       (keep["nk_hi"][:, :], keep["nk_lo"][:, :]), True, True)
                    last.then_inc(null_ready, 1)

                query_rows(0)
                queries(0)
                key_rows(0)
                null_scores(0)
                keys_values(0)

                def pair(u, p):
                    def scores(c):
                        if c >= 2:
                            pe.wait_ge(scores_biased, p * NG + c - 1)
                        for n in range(GH):
                            r, g = divmod(c * GH + n, KO)
                            rows = slice(r * DH, (r + 1) * DH)
                            last = matmul3(nc, b_s[c % 2][:, n * P:(n + 1) * P], (qT_hi[rows, g, :], qT_lo[rows, g, :]),
                                           (kT_hi[rows, :], kT_lo[rows, :]), True, True)
                        last.then_inc(scores_ready, 1)

                    def turned(c):
                        if c >= 1:
                            pe.wait_ge(pT_lo_ready, p * NG + c)
                        turn(b_pT, lambda k: sc[:, c * GH + k, :], GH, probs_ready, p * NG + c + 1, pT_ready)

                    def products(c):
                        pe.wait_ge(pT_lo_ready, p * NG + c + 1)
                        pe.wait_ge(acc_ready, p * NG + c)
                        for n in range(GH):
                            h = c * GH + n
                            last = matmul3(nc, b_pv[:, n * VW:(n + 1) * VW], (pT_hi[:, h, :], pT_lo[:, h, :]),
                                           (keep["v_hi"][:, :], keep["v_lo"][:, :]), True, True)
                        last.then_inc(pv_ready, 1)

                    pe.wait_ge(kT_ready, p + 1)
                    for c in range(NG):
                        scores(c)
                    turned(0)
                    key_rows(p + 1)
                    turned(1)
                    pe.wait_ge(v_ready, p + 1)
                    products(0)
                    turned(2)
                    products(1)
                    turned(3)
                    products(2)
                    keys_values(p + 1)
                    products(3)

                def tile(u, end):
                    for a in range(2):
                        turn(b_oT[a], lambda k, a=a: o[:, :, :].rearrange("p h d -> p (h d)")
                             [:, (4 * a + k) * P:(4 * a + k + 1) * P], 4, o_ready, u + 1, oT_ready)
                    query_rows(u + 1)
                    pe.wait_ge(oT_lo_ready, 2 * u + 2)
                    for k in range(KO):
                        last = matmul3(nc, b_o[:, :], (oT_hi[:, k, :], oT_lo[:, k, :]),
                                       (keep["wo_hi"][:, k, :], keep["wo_lo"][:, k, :]), k == 0, k == KO - 1)
                    last.then_inc(proj_ready, 1)
                    queries(u + 1)
                    null_scores(u + 1)
                    turn(b_xnT, lambda k: xn[:, k * P:(k + 1) * P], KD, xn_ready, u + 1, xnT_ready)
                    pe.wait_ge(xnT_copied, u + 1)
                    for k in range(KD):
                        last = nc.tensor.matmul(b_logit[:, 0:E], xnT[:, k, :], keep["router_wT"][:, k, :],
                                                start=(k == 0), stop=(k == KD - 1))
                    last.then_inc(logit_ready, 1)

                tiles(pe, pair, tile)


def route(nc, ctx, io, keep):
    J = NT // (P // E)
    L = P // E
    W = J * P
    with ExitStack() as scope:
        def sb(name, shape, dt=F32):
            return scope.enter_context(nc.sbuf_tensor("route_" + name, shape, dt))

        def sem(name):
            return ctx.enter_context(nc.semaphore("route_" + name))

        def bank(name):
            return scope.enter_context(nc.psum_tensor("route_" + name, [P, 512], F32))

        lg = sb("lg", [P, J, L, E])
        gate = sb("gate", [P, J, L, E])
        stand_in = sb("stand_in", [P, J, L, E])
        unseen = sb("unseen", [P, NT])
        row_max = sb("row_max", [P, NT])
        row_sum = sb("row_sum", [P, NT])
        val = sb("val", [P, W])
        flag = sb("flag", [P, W])
        greater = sb("greater", [P, W])
        equal = sb("equal", [P, W])
        rank = sb("rank", [P, W])
        zero = sb("zero", [P, W])
        count = sb("count", [P, 1])
        cand = sb("cand", [P, 1], I32)
        undo = sb("undo", [P, 1], I32)
        bit_f = sb("bit_f", [P, 1])
        bit_i = sb("bit_i", [P, 1], I32)
        need = sb("need", [P, 1])
        same_i = sb("same_i", [P, P], I32)
        same = sb("same", [P, P])
        before = sb("before", [P, P])
        taken = sb("taken", [P, J, L, E])
        pos_f = sb("pos_f", [P, EP, NT])
        pos_i = sb("pos_i", [P, EP, NT], I32)
        pos_p = sb("pos_p", [P, EP, NT], I32)
        tile_id = sb("tile_id_r", [P, NT])
        part_id = sb("part_id_r", [P, 1])
        source = sb("source", [P, NT])
        meta = sb("meta", [P, NT, META])
        b_val = [bank("b_val0"), bank("b_val1")]
        b_pos = [bank("b_pos0"), bank("b_pos1")]
        b_cnt, b_gt, b_eq, b_sel = bank("b_cnt"), bank("b_gt"), bank("b_eq"), bank("b_sel")

        lg_ready, val_turned, val_ready = sem("lg_ready"), sem("val_turned"), sem("val_ready")
        iota_ready, same_int, same_ready, before_ready = (
            sem("iota_ready"), sem("same_int"), sem("same_ready"), sem("before_ready"))
        counted, summed, exp_ready, shifted = sem("counted"), sem("summed"), sem("exp_ready"), sem("shifted")
        gt_counted, eq_counted, sel_counted = sem("gt_counted"), sem("eq_counted"), sem("sel_counted")
        gt_summed, eq_summed, sel_summed = sem("gt_summed"), sem("eq_summed"), sem("sel_summed")
        pos_ready, pos_turned, meta_ready, meta_out = (
            sem("pos_ready"), sem("pos_turned"), sem("meta_ready"), sem("meta_out"))
        r_step, r_bit = sem("r_step"), sem("r_bit")
        BITS = 31

        def by_tile(ap):
            return ap.rearrange("p (l j) e -> p j l e", j=J)

        def by_tile1(ap):
            return ap.rearrange("p (l j) -> p j l", j=J)

        def over_experts(ap):
            return by_tile1(ap).unsqueeze(3).to_broadcast([P, J, L, E])

        with nc.Block() as block:
            @block.gpsimd
            def _(pool):
                pool.iota(same_i[:, :], [[1, P]], base=P, channel_multiplier=-1).then_inc(same_int, 1)
                pool.iota(tile_id[:, :], [[1, NT]], base=0, channel_multiplier=0,
                          allow_small_or_imprecise_dtypes=True).then_inc(iota_ready, 1)
                pool.iota(part_id[:, :], [[1, 1]], base=0, channel_multiplier=1,
                          allow_small_or_imprecise_dtypes=True).then_inc(iota_ready, 1)
                pool.iota(keep["ids_a"][:, :], [[1, 16]], base=0, channel_multiplier=0,
                          allow_small_or_imprecise_dtypes=True).then_inc(iota_ready, 1)
                pool.iota(keep["ids_b"][:, :], [[1, 32]], base=0, channel_multiplier=0,
                          allow_small_or_imprecise_dtypes=True).then_inc(iota_ready, 1)
                pool.memset(zero[:, :], 0.0).then_inc(iota_ready, 1)
                pool.memset(meta[:, :, :], 0.0).then_inc(iota_ready, 1)
                pool.memset(pos_f[:, E:EP, :], -1.0).then_inc(iota_ready, 1)
                pool.wait_ge(same_ready, 1)
                pool.affine_select(out=before[:, :], in_=same[:, :], compare_op=ALU.is_gt, fill=0.0, base=0,
                                   pattern=[[1, P]], channel_multiplier=-1).then_inc(before_ready, 1)

            @block.tensor
            def _(pe):
                pe.wait_ge(lg_ready, 1)
                for j in range(J):
                    last = nc.tensor.transpose(b_val[j // 4][:, (j % 4) * P:(j % 4 + 1) * P],
                                               lg[:, j, :, :].rearrange("p l e -> p (l e)"), keep["ident"][:, :])
                last.then_inc(val_turned, 1)
                pe.wait_ge(same_ready, 1)
                with pe.Fori(0, BITS + 1) as i:
                    pe.wait_ge(counted, i + 1)
                    nc.tensor.matmul(b_cnt[:, 0:1], same[:, :], count[:, :], start=True, stop=True).then_inc(summed, 1)
                pe.wait_ge(gt_counted, 1)
                nc.tensor.matmul(b_gt[:, 0:1], same[:, :], count[:, :], start=True, stop=True).then_inc(gt_summed, 1)
                pe.wait_ge(before_ready, 1)
                pe.wait_ge(eq_counted, 1)
                nc.tensor.matmul(b_eq[:, 0:1], before[:, :], rank[:, W - 1:W], start=True, stop=True).then_inc(eq_summed, 1)
                pe.wait_ge(sel_counted, 1)
                nc.tensor.matmul(b_sel[:, 0:1], before[:, :], rank[:, W - 1:W], start=True, stop=True).then_inc(sel_summed, 1)
                pe.wait_ge(pos_ready, 1)
                for j in range(J):
                    last = nc.tensor.transpose(b_pos[j // 4][:, (j % 4) * P:(j % 4 + 1) * P],
                                               flag[:, j * P:(j + 1) * P], keep["ident"][:, :])
                last.then_inc(pos_turned, 1)

            @block.scalar
            def _(act):
                act.wait_ge(val_turned, 1)
                for a in range(2):
                    last = nc.scalar.activation(val[:, a * 512:(a + 1) * 512], b_val[a][:, :], ACT.Copy)
                last.then_inc(val_ready, 1)
                act.wait_ge(shifted, 1)
                nc.scalar.activation(gate[:, :, :, :], gate[:, :, :, :], ACT.Exp).then_inc(exp_ready, 1)

            @block.vector
            def _(dve):
                step = Count(dve, r_step)
                logits = by_tile(keep["logits"][:, 0:NT, :])
                none = keep["logits"][:, NONE, :].unsqueeze(1).unsqueeze(1).to_broadcast([P, J, L, E])
                step.step(nc.vector.tensor_scalar(unseen[:, :], keep["seen"][:, :], -1.0, 1.0, ALU.mult, ALU.add))
                step.inc(nc.vector.tensor_tensor(lg[:, :, :, :], logits, over_experts(keep["seen"][:, :]), ALU.mult))
                step.step(nc.vector.tensor_tensor(stand_in[:, :, :, :], none, over_experts(unseen[:, :]), ALU.mult))
                nc.vector.tensor_tensor(lg[:, :, :, :], lg[:, :, :, :], stand_in[:, :, :, :], ALU.add).then_inc(lg_ready, 1)
                dve.wait_ge(same_int, 1)
                step.step(nc.vector.tensor_scalar(same_i[:, :], same_i[:, :], E - 1, None, ALU.bitwise_and))
                nc.vector.tensor_scalar(same[:, :], same_i[:, :], 0.0, None, ALU.is_equal).then_inc(same_ready, 1)
                dve.wait_ge(lg_ready, 1)
                rows = lg[:, :, :, :].rearrange("p j l e -> p (j l) e")
                gates = gate[:, :, :, :].rearrange("p j l e -> p (j l) e")
                step.step(nc.vector.tensor_reduce(row_max[:, :], rows, AX_X, ALU.max))
                nc.vector.tensor_tensor(gates, rows, spread(row_max[:, :], [P, NT, E]), ALU.subtract).then_inc(shifted, 1)

                def reach(limit):
                    nc.vector.tensor_scalar(flag[:, :], val[:, :], limit, None, ALU.is_ge, ALU.add,
                                            accum_out=count[:, :]).then_inc(counted, 1)

                dve.wait_ge(val_ready, 1)
                reach(0.0)
                step.inc(nc.vector.memset(bit_f[:, :], float(1 << (BITS - 1))))
                step.inc(nc.vector.memset(bit_i[:, :], 1 << (BITS - 2)))
                dve.wait_ge(summed, 1)
                step.step(nc.vector.tensor_scalar(undo[:, :], b_cnt[:, 0:1], float(CAP), -1.0, ALU.is_lt, ALU.mult))
                step.step(nc.vector.tensor_scalar(cand[:, :], undo[:, :], 1 << (BITS - 1), None, ALU.bitwise_xor))
                with dve.Fori(0, BITS) as i:
                    dve.wait_ge(r_bit, i * 4)
                    reach(cand[:, :].bitcast(F32))
                    dve.wait_ge(summed, i + 2)
                    nc.vector.tensor_scalar(undo[:, :], b_cnt[:, 0:1], float(CAP), bit_f[:, :], ALU.is_lt, ALU.mult)\
                        .then_inc(r_bit, 1)
                    dve.wait_ge(r_bit, i * 4 + 1)
                    nc.vector.scalar_tensor_tensor(cand[:, :], undo[:, :], bit_i[:, :], cand[:, :],
                                                   ALU.bitwise_xor, ALU.bitwise_xor).then_inc(r_bit, 1)
                    nc.vector.tensor_scalar(bit_f[:, :], bit_f[:, :], 0.5, None, ALU.mult).then_inc(r_bit, 1)
                    nc.vector.tensor_scalar(bit_i[:, :], bit_i[:, :], 1, None, ALU.logical_shift_right).then_inc(r_bit, 1)
                dve.wait_ge(r_bit, BITS * 4)
                limit = cand[:, :].bitcast(F32)

                nc.vector.tensor_scalar(greater[:, :], val[:, :], limit, None, ALU.is_gt, ALU.add,
                                        accum_out=count[:, :]).then_inc(gt_counted, 1)
                step.step(nc.vector.tensor_scalar(equal[:, :], val[:, :], limit, None, ALU.is_equal))
                dve.wait_ge(iota_ready, 7)
                nc.vector.tensor_tensor_scan(rank[:, :], equal[:, :], zero[:, :], 0.0, ALU.add, ALU.add)\
                    .then_inc(eq_counted, 1)
                dve.wait_ge(gt_summed, 1)
                step.step(nc.vector.tensor_scalar(need[:, :], b_gt[:, 0:1], -1.0, float(CAP), ALU.mult, ALU.add))
                dve.wait_ge(eq_summed, 1)
                step.step(nc.vector.tensor_tensor(need[:, :], need[:, :], b_eq[:, 0:1], ALU.subtract))
                step.step(nc.vector.scalar_tensor_tensor(flag[:, :], rank[:, :], need[:, :], equal[:, :],
                                                         ALU.is_le, ALU.mult))
                step.step(nc.vector.tensor_tensor(flag[:, :], flag[:, :], greater[:, :], ALU.add))
                nc.vector.tensor_tensor_scan(rank[:, :], flag[:, :], zero[:, :], 0.0, ALU.add, ALU.add)\
                    .then_inc(sel_counted, 1)
                dve.wait_ge(exp_ready, 1)
                step.step(nc.vector.tensor_reduce(row_sum[:, :], gates, AX_X, ALU.add))
                step.step(nc.vector.reciprocal(row_sum[:, :], row_sum[:, :]))
                step.inc(nc.vector.tensor_tensor(gates, gates, spread(row_sum[:, :], [P, NT, E]), ALU.mult))
                dve.wait_ge(sel_summed, 1)
                nc.vector.scalar_tensor_tensor(flag[:, :], rank[:, :], b_sel[:, 0:1], flag[:, :], ALU.add, ALU.mult)\
                    .then_inc(pos_ready, 1)
                step.step(nc.vector.tensor_scalar(source[:, :], tile_id[:, :], -float(NONE), None, ALU.add))
                step.step(nc.vector.tensor_tensor(source[:, :], source[:, :], keep["seen"][:, :], ALU.mult))
                step.step(nc.vector.tensor_scalar(source[:, :], source[:, :], float(NONE), float(P), ALU.add, ALU.mult))
                step.inc(nc.vector.tensor_scalar(meta[:, :, E].bitcast(I32), source[:, :], part_id[:, :], None, ALU.add))
                dve.wait_ge(pos_turned, 1)
                for a in range(2):
                    turned = b_pos[a][:, :].rearrange("p (j l e) -> p j l e", l=L, e=E)
                    js = slice(a * J // 2, (a + 1) * J // 2)
                    step.inc(nc.vector.tensor_scalar(taken[:, js, :, :], turned, 0.0, None, ALU.is_gt))
                    for j in range(J // 2):
                        out = pos_f[:, 0:E, :].rearrange("p e (l j) -> p j l e", j=J)[:, a * J // 2 + j, :, :]
                        step.inc(nc.vector.tensor_scalar(out, turned[:, j, :, :], -1.0, None, ALU.add))
                step.wait()
                step.step(nc.vector.tensor_tensor(gate[:, :, :, :], gate[:, :, :, :], taken[:, :, :, :], ALU.mult))
                step.step(nc.vector.tensor_reduce(row_sum[:, :], gates, AX_X, ALU.add))
                step.step(nc.vector.tensor_scalar(row_max[:, :], row_sum[:, :], 0.0, None, ALU.is_equal))
                step.step(nc.vector.tensor_tensor(row_sum[:, :], row_sum[:, :], row_max[:, :], ALU.add))
                step.step(nc.vector.reciprocal(row_sum[:, :], row_sum[:, :]))
                nc.vector.tensor_tensor(meta[:, :, 0:E].rearrange("p (l j) e -> p j l e", j=J), gate[:, :, :, :],
                                        row_sum[:, :].rearrange("p (j l) -> p j l", j=J).unsqueeze(3)
                                        .to_broadcast([P, J, L, E]), ALU.mult).then_inc(meta_ready, 1)
                step.step(nc.vector.tensor_copy(pos_i[:, :, :], pos_f[:, :, :]))
                step.step(nc.vector.tensor_scalar(pos_p[:, :, :], pos_i[:, :, :], 5, None, ALU.arith_shift_right))
                step.inc(nc.vector.tensor_copy(keep["pos_a"][:, :, :], pos_p[:, :, :]))
                step.step(nc.vector.tensor_scalar(pos_i[:, :, :], pos_i[:, :, :], 31, None, ALU.bitwise_and))
                step.inc(nc.vector.tensor_copy(keep["pos_b"][:, :, :], pos_i[:, :, :]))
                step.inc(nc.vector.tensor_copy(keep["tile_ids"][:, :], tile_id[:, :]))
                step.inc(nc.vector.tensor_copy(keep["part_id"][:, :], part_id[:, :]))
                step.wait()

            @block.sync
            def _(sp):
                sp.wait_ge(meta_ready, 1)
                sp.dma_start(keep["meta_dram"].rearrange("(t p) c -> p t c", p=P), meta[:, :, :]).then_inc(meta_out, 16)
                sp.wait_ge(meta_out, 16)


def experts(nc, ctx, io, keep):
    RING = 4
    HB = 2
    with ExitStack() as scope:
        def sb(name, shape, dt=F32):
            return scope.enter_context(nc.sbuf_tensor("experts_" + name, shape, dt))

        def sem(name):
            return ctx.enter_context(nc.semaphore("experts_" + name))

        def bank(name):
            return scope.enter_context(nc.psum_tensor("experts_" + name, [P, 512], F32))

        w_raw = sb("w_raw", [P, RING, 2 * D])
        w_hi = sb("w_hi", [P, RING, 2 * D], F32R)
        w_lo = sb("w_lo", [P, RING, 2 * D], F32R)
        h = sb("h", [P, HB, CAP])
        h_hi = sb("h_hi", [P, HB, CAP], F32R)
        h_lo = sb("h_lo", [P, HB, CAP], F32R)
        b1 = sb("b1_sb", [P, E, FT])
        b2 = sb("b2_sb", [P, E, D])
        hot_a = sb("hot_a", [P, NT, 16], BF16)
        hot_b = sb("hot_b", [P, NT, 32], BF16)
        named = sb("named", [P, NT, 2, 32], BF16)
        list_i = sb("list_i", [16, 32], I32)
        name_f = sb("name_f", [16, 32])
        next_ids = sb("next_ids", [P, CT], U32)
        ids = sb("ids", [P, CT], U32)
        rows_meta = sb("rows_meta", [P, CT, META])
        rows_id = sb("rows_id", [P, CT], U32)
        weight = sb("weight", [P, CT])
        rows = sb("rows", [P, CT, D])
        xT_hi = sb("xT_hi", [P, 2, KD, CAP], F32R)
        xT_lo = sb("xT_lo", [P, 2, KD, CAP], F32R)
        bias_w = sb("bias_w", [P, CT, D])
        y = sb("y_out", [P, CT, D])
        b_h = [bank("b_h0"), bank("b_h1")]
        b_y = [bank(f"b_y{c}") for c in range(CT)]
        b_list, b_x = bank("b_list"), bank("b_x")

        w_in = [sem(f"w_in{slot}") for slot in range(RING)]
        w_hi_ready, w_lo_ready = sem("w_hi_ready"), sem("w_lo_ready")
        bias_loaded = sem("bias_loaded")
        h_ready, h_done, h_hi_ready, h_lo_ready = sem("h_ready"), sem("h_done"), sem("h_hi_ready"), sem("h_lo_ready")
        y_ready, y_scaled, y_added = sem("yb_ready"), sem("y_scaled"), sem("y_added")
        hot_ready, list_summed, list_ready, list_moved = (
            sem("hot_ready"), sem("list_summed"), sem("list_ready"), sem("list_moved"))
        meta_in, rows_in, weight_ready, bias_ready = (
            sem("meta_in"), sem("rows_in"), sem("weight_ready"), sem("bias_w_ready"))
        ids_ready, rows_id_ready = sem("ids_ready"), sem("rows_id_ready")
        x_turned, x_hi_ready, x_lo_ready = sem("x_turned"), sem("x_hi_ready"), sem("x_lo_ready")
        f_hot, f_list, passed = sem("f_hot"), sem("f_list"), sem("f_passed")

        HOT, LIST, NAME, TURN = 0, 5, 6, 11

        with nc.Block() as block:
            @block.sync
            def _(sp):
                def load(chunk, slot):
                    sp.dma_start(w_raw[:, slot, :], io["w"][bass.ds(chunk, 1), :, :].rearrange("o p n -> p (o n)"))\
                        .then_inc(w_in[slot], 16)

                sp.dma_start(b1[:, :, :], io["b1"]).then_inc(bias_loaded, 16)
                for g in range(RING):
                    load(g, g)
                sp.dma_start(b2[:, :, :].rearrange("p e d -> p (e d)"), io["b2"].to_broadcast([P, E * D]))\
                    .then_inc(bias_loaded, 16)
                with sp.Fori(0, E * FT // RING - 1) as i:
                    for g in range(RING):
                        sp.wait_ge(w_lo_ready, i * RING + g + 1)
                        load(i * RING + (RING + g), g)
                for g in range(2):
                    sp.wait_ge(w_lo_ready, E * FT - RING + g + 1)
                    load(g, g)
                for g in range(2):
                    sp.wait_ge(w_in[g], (E * FT // RING + 1) * 16)
                sp.wait_ge(bias_loaded, 32)

            @block.gpsimd
            def _(pool):
                def fetch(n):
                    pool.wait_ge(list_ready, n + 1)
                    alone(pool, passed)
                    pool.dma_start(next_ids[:, :], list_i[:, :].bitcast(U32)).then_inc(list_moved, 16)
                    pool.wait_ge(list_moved, (n + 1) * 16)
                    alone(pool, passed)
                    for c in range(CT):
                        pool.indirect_dma_start(rows_meta[:, c, :], None, keep["meta_dram"],
                                                bass.IndirectOffsetOnAxis(next_ids[:, c:c + 1], 0)).then_inc(meta_in, 16)
                    pool.wait_ge(meta_in, (n + 1) * CT * 16)
                    alone(pool, passed)
                    nc.gpsimd.tensor_copy(rows_id[:, :], rows_meta[:, :, E].bitcast(U32)).then_inc(rows_id_ready, 1)
                    pool.wait_ge(rows_id_ready, n + 1)
                    pool.wait_ge(x_turned, n * KD)
                    alone(pool, passed)
                    for c in range(CT):
                        pool.indirect_dma_start(rows[:, c, :], None, keep["xn_dram"],
                                                bass.IndirectOffsetOnAxis(rows_id[:, c:c + 1], 0)).then_inc(rows_in, 16)

                def adopt(n):
                    nc.gpsimd.tensor_copy(ids[:, :], next_ids[:, :]).then_inc(ids_ready, 1)
                    nc.gpsimd.tensor_copy(weight[:, :], rows_meta[:, :, bass.ds(n, 1)].rearrange("p c o -> p (c o)"))\
                        .then_inc(weight_ready, 1)
                    pool.wait_ge(weight_ready, n + 1)
                    alone(pool, passed)
                    for c in range(CT):
                        nc.gpsimd.tensor_tensor(bias_w[:, c, :], b2[:, bass.ds(n, 1), :].rearrange("p o d -> p (o d)"),
                                                weight[:, c:c + 1].to_broadcast([P, D]), ALU.mult).then_inc(bias_ready, 1)

                def add_rows(n):
                    pool.wait_ge(ids_ready, n + 1)
                    for c in range(CT):
                        pool.wait_ge(y_scaled, n * CT + c + 1)
                        alone(pool, passed)
                        pool.indirect_dma_start(io["out"], bass.IndirectOffsetOnAxis(ids[:, c:c + 1], 0), y[:, c, :],
                                                None, compute_op=ALU.add).then_inc(y_added, 16)

                pool.wait_ge(bias_loaded, 32)
                pool.wait_ge(keep["x_copied"], 16)
                fetch(0)
                with pool.Fori(0, E) as e:
                    pool.wait_ge(y_added, e * CT * 16)
                    alone(pool, passed)
                    adopt(e)
                    pool.wait_ge(weight_ready, e + 1)
                    pool.wait_ge(ids_ready, e + 1)
                    fetch(e + 1)
                    add_rows(e)
                pool.wait_ge(y_added, E * CT * 16)
                pool.wait_ge(rows_in, (E + 1) * CT * 16)

            @block.scalar
            def _(act):
                def split(turns, slot):
                    act.wait_ge(w_in[slot], (turns + 1) * 16)
                    nc.scalar.activation(w_hi[:, slot, :], w_raw[:, slot, :], ACT.Copy).then_inc(w_hi_ready, 1)

                def turned(n, k, side):
                    act.wait_ge(x_turned, n * KD + k + 1)
                    nc.scalar.activation(xT_hi[:, bass.ds(side, 1), k, :].rearrange("p o c -> p (o c)"), b_x[:, :],
                                         ACT.Copy).then_inc(x_hi_ready, 1)

                split(0, 0)
                split(0, 1)
                for k in range(KD):
                    turned(0, k, 0)
                act.wait_ge(bias_loaded, 32)
                with act.Fori(0, E) as e:
                    side = act.snap((e + 1) % 2)
                    for f in range(FT):
                        g = e * FT + f
                        act.wait_ge(h_ready, g + 1)
                        nc.scalar.activation(h[:, f % HB, :], b_h[f % 2][:, :], ACT.Gelu,
                                             bias=b1[:, bass.ds(e, 1), f].rearrange("p o -> p o")).then_inc(h_done, 1)
                        act.wait_ge(h_done, g + 1)
                        nc.scalar.activation(h_hi[:, f % HB, :], h[:, f % HB, :], ACT.Copy).then_inc(h_hi_ready, 1)
                        split(e * (FT // RING) + (f + 2) // RING, (f + 2) % RING)
                        if TURN <= f < TURN + KD:
                            turned(e + 1, f - TURN, side)

            @block.vector
            def _(dve):
                def split(g, slot):
                    dve.wait_ge(w_hi_ready, g + 1)
                    nc.vector.tensor_tensor(w_lo[:, slot, :], w_raw[:, slot, :], f32(w_hi[:, slot, :]), ALU.subtract)\
                        .then_inc(w_lo_ready, 1)

                def hot(n, part):
                    if part == 0:
                        dve.wait_ge(list_summed, n)
                        nc.vector.tensor_tensor(hot_a[:, :, :], keep["pos_a"][:, bass.ds(n, 1), :]
                                                .rearrange("p o t -> p (o t)").unsqueeze(2).to_broadcast([P, NT, 16]),
                                                keep["ids_a"][:, :].unsqueeze(1).to_broadcast([P, NT, 16]),
                                                ALU.is_equal).then_inc(f_hot, 1)
                    elif part == 1:
                        nc.vector.tensor_tensor(hot_b[:, :, :], keep["pos_b"][:, bass.ds(n, 1), :]
                                                .rearrange("p o t -> p (o t)").unsqueeze(2).to_broadcast([P, NT, 32]),
                                                keep["ids_b"][:, :].unsqueeze(1).to_broadcast([P, NT, 32]),
                                                ALU.is_equal).then_inc(f_hot, 1)
                    elif part == 2:
                        dve.wait_ge(f_hot, n * 3 + 2)
                        nc.vector.tensor_tensor(named[:, :, 0, :], hot_b[:, :, :],
                                                spread(keep["tile_ids"][:, :], [P, NT, 32]), ALU.mult).then_inc(f_hot, 1)
                    else:
                        dve.wait_ge(f_hot, n * 3 + 3)
                        nc.vector.tensor_scalar(named[:, :, 1, :], hot_b[:, :, :], keep["part_id"][:, :], None,
                                                ALU.mult).then_inc(hot_ready, 1)

                def name(n):
                    dve.wait_ge(list_summed, n + 1)
                    nc.vector.tensor_copy(name_f[:, :], b_list[0:16, 32:64]).then_inc(f_list, 1)
                    dve.wait_ge(f_list, n + 1)
                    dve.wait_ge(list_moved, n * 16)
                    nc.vector.scalar_tensor_tensor(list_i[:, :], b_list[0:16, 0:32], float(P), name_f[:, :],
                                                   ALU.mult, ALU.add).then_inc(list_ready, 1)

                def turned(n, k, side):
                    dve.wait_ge(x_hi_ready, n * KD + k + 1)
                    nc.vector.tensor_tensor(xT_lo[:, bass.ds(side, 1), k, :].rearrange("p o c -> p (o c)"), b_x[:, :],
                                            f32(xT_hi[:, bass.ds(side, 1), k, :]).rearrange("p o c -> p (o c)"),
                                            ALU.subtract).then_inc(x_lo_ready, 1)

                def scale_rows(n):
                    dve.wait_ge(bias_ready, (n + 1) * CT)
                    dve.wait_ge(y_added, n * CT * 16)
                    for c in range(CT):
                        dve.wait_ge(y_ready, n * CT + c + 1)
                        nc.vector.scalar_tensor_tensor(y[:, c, :], b_y[c][:, :], weight[:, c:c + 1], bias_w[:, c, :],
                                                       ALU.mult, ALU.add).then_inc(y_scaled, 1)

                for part in range(4):
                    hot(0, part)
                name(0)
                split(0, 0)
                split(1, 1)
                for k in range(KD):
                    turned(0, k, 0)
                with dve.Fori(0, E) as e:
                    side = dve.snap((e + 1) % 2)
                    for f in range(FT):
                        g = e * FT + f
                        dve.wait_ge(h_hi_ready, g + 1)
                        nc.vector.tensor_tensor(h_lo[:, f % HB, :], h[:, f % HB, :], f32(h_hi[:, f % HB, :]),
                                                ALU.subtract).then_inc(h_lo_ready, 1)
                        split(g + 2, (f + 2) % RING)
                        if HOT <= f < HOT + 4:
                            hot(e + 1, f - HOT)
                        if f == NAME:
                            name(e + 1)
                        if TURN <= f < TURN + KD:
                            turned(e + 1, f - TURN, side)
                    scale_rows(e)

            @block.tensor
            def _(pe):
                def make_list(n):
                    pe.wait_ge(hot_ready, n + 1)
                    for t in range(NT):
                        last = nc.tensor.matmul(b_list[0:16, 0:64], hot_a[:, t, :],
                                                named[:, t, :, :].rearrange("p a b -> p (a b)"),
                                                start=(t == 0), stop=(t == NT - 1))
                    last.then_inc(list_summed, 1)

                def turn(n, k):
                    if k == 0:
                        pe.wait_ge(rows_in, (n + 1) * CT * 16)
                    pe.wait_ge(x_lo_ready, n * KD + k)
                    for c in range(CT):
                        last = nc.tensor.transpose(b_x[:, c * P:(c + 1) * P], rows[:, c, k * P:(k + 1) * P],
                                                   keep["ident"][:, :])
                    last.then_inc(x_turned, 1)

                def fc1(g, f, sides):
                    pe.wait_ge(w_lo_ready, g + 1)
                    for k in range(KD):
                        cols = slice(k * P, (k + 1) * P)
                        last = matmul3(nc, b_h[f % 2][:, :], (w_hi[:, f % RING, cols], w_lo[:, f % RING, cols]),
                                       sides[k], k == 0, k == KD - 1)
                    last.then_inc(h_ready, 1)

                def fc2(e, g, f):
                    pe.wait_ge(h_lo_ready, g + 1)
                    for c in range(CT):
                        if f == 0 and c == 0:
                            pe.wait_ge(y_scaled, e * CT)
                        cols = slice(c * P, (c + 1) * P)
                        last = matmul3(nc, b_y[c][:, :], (h_hi[:, f % HB, cols], h_lo[:, f % HB, cols]),
                                       (w_hi[:, f % RING, D:2 * D], w_lo[:, f % RING, D:2 * D]), f == 0, f == FT - 1)
                        if f == FT - 1:
                            last.then_inc(y_ready, 1)

                make_list(0)
                for k in range(KD):
                    turn(0, k)
                with pe.Fori(0, E) as e:
                    side = pe.snap(e % 2)
                    pe.wait_ge(x_lo_ready, (e + 1) * KD)
                    sides = [(xT_hi[:, bass.ds(side, 1), k, :].rearrange("p o c -> p (o c)"),
                              xT_lo[:, bass.ds(side, 1), k, :].rearrange("p o c -> p (o c)")) for k in range(KD)]
                    for f in range(FT):
                        g = e * FT + f
                        fc1(g, f, sides)
                        if f > 0:
                            fc2(e, g - 1, f - 1)
                        if f == LIST:
                            make_list(e + 1)
                        if TURN <= f < TURN + KD:
                            turn(e + 1, f - TURN)
                    fc2(e, e * FT + FT - 1, FT - 1)


def program(nc, io):
    ctx = ExitStack()
    with ctx:
        def sb(name, shape, dt=F32):
            return ctx.enter_context(nc.sbuf_tensor(name, shape, dt))

        keep = {
            "ident": sb("ident", [P, P]),
            "logits": sb("logits", [P, NT + 1, E]),
            "seen": sb("seen_tiles", [P, NT]),
            "pos_a": sb("pos_a", [P, EP, NT], BF16),
            "pos_b": sb("pos_b", [P, EP, NT], BF16),
            "ids_a": sb("ids_a", [P, 16], BF16), "ids_b": sb("ids_b", [P, 32], BF16),
            "tile_ids": sb("tile_ids", [P, NT], BF16), "part_id": sb("part_id", [P, 1]),
            "x_copied": ctx.enter_context(nc.semaphore("x_copied")),
            "xn_filled": ctx.enter_context(nc.semaphore("xn_filled")),
            "xn_dram": nc.dram_tensor("xn_dram", [(NT + 1) * P, D], F32).ap(),
            "meta_dram": nc.dram_tensor("meta_dram", [N, META], F32).ap(),
            "ql_dram": nc.dram_tensor("ql_dram", [P, QCOLS], I32).ap(),
            "kl_dram": nc.dram_tensor("kl_dram", [NPAIR, KCOLS], I32).ap(),
        }
        with ExitStack() as scope:
            def sa(name, shape, dt=F32):
                return scope.enter_context(nc.sbuf_tensor(name, shape, dt))

            keep |= {
                "half": sa("half", [P, 1]),
                "causal": sa("causal", [P, 2, P]),
                "hidden": sa("hidden", [P, NT + 1, P], BF16),
                "has_key": sa("has_key", [P, NT]),
                "ql": sa("ql_row", [1, P * QCOLS], I32),
                "kl": sa("kl_row", [1, NPAIR * KCOLS], I32),
                "wq_hi": sa("wq_hi", [P, KD, H * DH], F32R), "wq_lo": sa("wq_lo", [P, KD, H * DH], F32R),
                "wkv_hi": sa("wkv_hi", [P, KD, 3 * DH], F32R), "wkv_lo": sa("wkv_lo", [P, KD, 3 * DH], F32R),
                "wo_hi": sa("wo_hi", [P, KO, D], F32R), "wo_lo": sa("wo_lo", [P, KO, D], F32R),
                "nk_hi": sa("nk_hi", [P, 2], F32R), "nk_lo": sa("nk_lo", [P, 2], F32R),
                "v_hi": sa("v_hi", [P, VW], F32R), "v_lo": sa("v_lo", [P, VW], F32R),
                "null_v": sa("null_v_row", [P, VW]), "null_bias": sa("null_bias_row", [P, H]),
                "g_in": sa("g_in_row", [P, D]), "g_out": sa("g_out_row", [P, D]), "norm_w": sa("norm_w_row", [P, D]),
                "router_b": sa("router_b_row", [P, E]), "router_wT": sa("router_wT_sb", [P, KD, E]),
            }
            make_lists(nc, ctx, io, keep)
            attend(nc, ctx, io, keep)
        route(nc, ctx, io, keep)
        experts(nc, ctx, io, keep)


def kernel(x, fside_16xSxS_0, cond_64, mask_BxS_bk0, L0_cond_g_in, L0_cond_null_attn_bias, L0_cond_Wq,
           L0_cond_Wkv, L0_cond_Wo, L0_cond_g_out, L0_ffn_norm_weight, L0_ffn_router_weight,
           L0_ffn_router_bias, L0_ffn_fc1_weight, L0_ffn_fc1_bias, L0_ffn_fc2_weight, L0_ffn_fc2_bias):
    import numpy as np

    import concourse.bacc as bacc
    from concourse.bass_utils import run_bass_kernel_spmd

    a = np.asarray
    order = [2 * (n % KO) + n // KO for n in range(H)]
    wkv = a(L0_cond_Wkv)
    wk, wv = wkv[:, :DH], wkv[:, DH:]
    cond = a(cond_64)
    nk = np.zeros((P, 2), np.float32)
    nk[:DH, 0] = nk[DH:, 1] = cond[0]
    w1 = a(L0_ffn_fc1_weight).reshape(E, FT, P, KD, P).transpose(0, 1, 4, 3, 2).reshape(E, FT, P, D)
    w2 = a(L0_ffn_fc2_weight).reshape(E, D, FT, P).transpose(0, 2, 3, 1)
    arrays = {
        "x": a(x).reshape(N, D),
        "bias": a(fside_16xSxS_0)[order].reshape(H, QT, P, QT, P).transpose(1, 3, 2, 0, 4).reshape(QT * QT * P, H * P),
        "mask": a(mask_BxS_bk0).reshape(1, N),
        "wq": a(L0_cond_Wq).reshape(KD, P, H * DH).transpose(1, 0, 2),
        "wkv": np.concatenate([wk, wk, wv], 1).reshape(KD, P, 3 * DH).transpose(1, 0, 2),
        "wo": a(L0_cond_Wo).reshape(H, DH, D)[order].reshape(KO, P, D).transpose(1, 0, 2),
        "nk": nk,
        "null_v": np.concatenate([cond[1], np.ones(1, np.float32), np.zeros(1, np.float32)]).reshape(1, VW),
        "null_bias": a(L0_cond_null_attn_bias)[order].reshape(1, H),
        "g_in": a(L0_cond_g_in).reshape(1, D), "g_out": a(L0_cond_g_out).reshape(1, D),
        "norm_w": a(L0_ffn_norm_weight).reshape(1, D),
        "router_wT": a(L0_ffn_router_weight).reshape(E, KD, P).transpose(2, 1, 0),
        "router_b": a(L0_ffn_router_bias).reshape(1, E),
        "w": np.concatenate([w1, w2], 3).reshape(E * FT, P, 2 * D),
        "b1": a(L0_ffn_fc1_bias).reshape(E, FT, P).transpose(2, 0, 1),
        "b2": a(L0_ffn_fc2_bias).reshape(1, E * D),
    }
    arrays = {name: np.ascontiguousarray(v) for name, v in arrays.items()}
    nc = bacc.Bacc("TRN2", target_bir_lowering=False, num_devices=1)
    io = {name: nc.dram_tensor("in_" + name, v.shape, mybir.dt.from_np(v.dtype), kind="ExternalInput").ap()
          for name, v in arrays.items()}
    io["out"] = nc.dram_tensor("out", (N, D), F32, kind="ExternalOutput").ap()
    program(nc, io)
    got = run_bass_kernel_spmd(nc, [{"in_" + name: v for name, v in arrays.items()}], core_ids=[0])
    return got.results[0]["out"].reshape(B, S, D)
```

```python
from contextlib import ExitStack

import concourse.bass as bass
import concourse.mybir as mybir
from concourse.alu_op_type import AluOpType as ALU

F32 = mybir.dt.float32
F32R = mybir.dt.float32r
BF16 = mybir.dt.bfloat16
I32 = mybir.dt.int32
U32 = mybir.dt.uint32
U8 = mybir.dt.uint8
ACT = mybir.ActivationFunctionType
AX_X = mybir.AxisListType.X

P = 128
B, S, D = 16, 512, 512
H, DH = 16, 64
E, F = 16, 2048
N = B * S
NT = N // P
QT = S // P
KD = D // P
KO = H * DH // P
CAP = N // E
CT = CAP // P
FT = F // P
GH = 4
NG = H // GH
VW = DH + 2
SCALE = DH ** -0.5
EPS = 1e-5
MASKED = -1e30
NONE = NT
KCOLS = 8
NPAIR = 256
EP = E + 2
META = 32


class Count:

    def __init__(self, eng, sem, base=0):
        self.eng, self.sem, self.base, self.n = eng, sem, base, 0

    def inc(self, instruction):
        instruction.then_inc(self.sem, 1)
        self.n += 1

    def wait(self):
        self.eng.wait_ge(self.sem, self.base + self.n)

    def step(self, instruction):
        self.inc(instruction)
        self.wait()


def f32(ap):
    return ap.bitcast(F32)


def spread(ap, shape):
    return ap.unsqueeze(len(ap.shape)).to_broadcast(shape)


def alone(eng, passed):
    eng.sem_inc(passed, 1)


def make_lists(nc, ctx, io, keep):
    with ExitStack() as scope:
        def sb(name, shape, dt=F32):
            return scope.enter_context(nc.sbuf_tensor("lists_" + name, shape, dt))

        def sem(name):
            return ctx.enter_context(nc.semaphore("lists_" + name))

        mask8 = sb("mask8", [P, N], U8)
        wq_raw = sb("wq_raw", [P, KD, H * DH])
        wo_raw = sb("wo_raw", [P, KO, D])
        wkv_raw = sb("wkv_raw", [P, KD, 3 * DH])
        seen = sb("seen", [P, NT])
        seen_pair = sb("seen_pair", [P, NT, QT])
        tri = sb("tri", [P, QT, QT])
        zero = sb("zero", [P, NT * QT])
        rank_k = sb("rank_k", [P, NT * QT])
        slot = sb("slot", [P, 2])
        first = sb("first", [P, 1])
        key_tile = sb("key_tile", [P, NT * QT])
        bias_tile = sb("bias_tile", [P, NT * QT])
        off_diag = sb("off_diag", [P, NT * QT])
        query_tile = sb("query_tile", [P, NT * QT])
        carry = sb("carry", [P, NT * QT])
        diag = sb("diag", [P, NT * QT])
        begin = sb("begin", [P, NT])
        hit_k = sb("hit_k", [P, 2, NT * QT])
        junk = sb("junk", [P, NT * QT])
        kl = sb("kl", [P, 2, KCOLS])
        kl_i = sb("kl_i", [P, 2, KCOLS], I32)

        mask_in, raw_in = sem("mask_in"), sem("raw_in")
        const_in = sem("const_in")
        iotas_done, slots_done, ident_done = sem("iotas_done"), sem("slots_done"), sem("ident_done")
        hi_done, hidden_done = sem("hi_done"), sem("hidden_done")
        setup_step, lists_done, lists_out, lists_in = (
            sem("setup_step"), sem("lists_done"), sem("lists_out"), sem("lists_in"))
        splits = ((wkv_raw, keep["wkv_hi"], keep["wkv_lo"]), (wq_raw, keep["wq_hi"], keep["wq_lo"]),
                  (wo_raw, keep["wo_hi"], keep["wo_lo"]))

        with nc.Block() as block:
            @block.sync
            def _(sp):
                sp.dma_start(mask8[:, :], io["mask"].to_broadcast([P, N])).then_inc(mask_in, 16)
                sp.dma_start(keep["null_k"][:, :], io["null_k"].to_broadcast([P, DH])).then_inc(const_in, 16)
                for name in ("g_in", "g_out", "norm_w"):
                    sp.dma_start(keep[name][:, :], io[name].to_broadcast([P, D])).then_inc(const_in, 16)
                sp.dma_start(keep["null_bias"][:, :], io["null_bias"].to_broadcast([P, H])).then_inc(const_in, 16)
                sp.dma_start(keep["router_b"][:, :], io["router_b"].to_broadcast([P, E])).then_inc(const_in, 16)
                sp.dma_start(keep["null_v"][:, :], io["null_v"].to_broadcast([P, VW])).then_inc(const_in, 16)
                sp.dma_start(keep["router_wT"][:, :, :], io["router_wT"]).then_inc(const_in, 16)
                sp.dma_start(wkv_raw[:, :, :], io["wkv"]).then_inc(raw_in, 16)
                sp.dma_start(wq_raw[:, :, :], io["wq"]).then_inc(raw_in, 16)
                sp.dma_start(wo_raw[:, :, :], io["wo"]).then_inc(raw_in, 16)
                sp.wait_ge(lists_done, 1)
                sp.dma_start(keep["kl_dram"].rearrange("(a p) c -> p a c", p=P), kl_i[:, :, :]).then_inc(lists_out, 16)
                sp.wait_ge(lists_out, 16)
                sp.dma_start(keep["kl"][:, :], keep["kl_dram"].rearrange("(o p) c -> o (p c)", o=1)).then_inc(lists_in, 16)
                sp.wait_ge(lists_in, 16)

            @block.gpsimd
            def _(pool):
                ident = keep["ident"]
                pool.iota(slot[:, :], [[P, 2]], base=0, channel_multiplier=1,
                          allow_small_or_imprecise_dtypes=True).then_inc(slots_done, 1)
                pool.iota(query_tile[:, :], [[1, NT], [0, QT]], base=0, channel_multiplier=0,
                          allow_small_or_imprecise_dtypes=True).then_inc(iotas_done, 1)
                pool.iota(key_tile[:, :], [[QT, B], [0, QT], [1, QT]], base=0, channel_multiplier=0,
                          allow_small_or_imprecise_dtypes=True).then_inc(iotas_done, 1)
                pool.iota(bias_tile[:, :], [[0, B], [QT, QT], [1, QT]], base=0, channel_multiplier=0,
                          allow_small_or_imprecise_dtypes=True).then_inc(iotas_done, 1)
                pool.iota(off_diag[:, :], [[0, B], [1, QT], [-1, QT]], base=0, channel_multiplier=0,
                          allow_small_or_imprecise_dtypes=True).then_inc(iotas_done, 1)
                pool.memset(ident[:, :], 0.0).then_inc(ident_done, 1)
                pool.memset(keep["causal"][:, :, :], 0.0).then_inc(ident_done, 1)
                pool.memset(keep["half"][:, :], -0.5).then_inc(ident_done, 1)
                pool.wait_ge(ident_done, 3)
                pool.affine_select(out=ident[:, :], in_=ident[:, :], compare_op=ALU.not_equal, fill=1.0,
                                   base=0, pattern=[[-1, P]], channel_multiplier=1).then_inc(ident_done, 1)
                pool.affine_select(out=keep["causal"][:, 1, :], in_=keep["causal"][:, 1, :],
                                   compare_op=ALU.is_ge, fill=MASKED, base=0, pattern=[[-1, P]],
                                   channel_multiplier=1).then_inc(ident_done, 1)
                pool.wait_ge(ident_done, 5)

            @block.scalar
            def _(act):
                act.wait_ge(mask_in, 16)
                nc.scalar.activation(keep["hidden"][:, 0:NT, :], mask8[:, :].rearrange("p (t j) -> p t j", j=P),
                                     ACT.Copy, bias=MASKED, scale=-MASKED).then_inc(hidden_done, 1)
                act.wait_ge(raw_in, 48)
                for raw, hi, _ in splits:
                    nc.scalar.activation(hi[:], raw[:], ACT.Copy).then_inc(hi_done, 1)
                act.wait_ge(hidden_done, 1)

            @block.vector
            def _(dve):
                step = Count(dve, setup_step)
                dve.wait_ge(const_in, 8 * 16)
                step.inc(nc.vector.tensor_scalar(keep["null_bias"][:, :], keep["null_bias"][:, :], -1.0, None, ALU.mult))
                step.inc(nc.vector.memset(keep["hidden"][:, NT, :], MASKED))
                step.inc(nc.vector.memset(keep["logits"][:, :, :], 0.0))
                step.inc(nc.vector.memset(zero[:, :], 0.0))
                step.inc(nc.vector.memset(keep["v_hi"][:, DH:DH + 1].bitcast(F32), 1.0))
                step.inc(nc.vector.memset(keep["v_hi"][:, DH + 1:VW].bitcast(F32), 0.0))
                step.inc(nc.vector.memset(keep["v_lo"][:, DH:VW].bitcast(F32), 0.0))
                step.step(nc.vector.memset(tri[:, :, :], 1.0))
                for q in range(QT - 1):
                    step.inc(nc.vector.memset(tri[:, q, q + 1:QT], 0.0))
                has = keep["has_key"]
                seen4 = seen[:, :].rearrange("p (b q) -> p b q", q=QT)
                has4 = has[:, :].rearrange("p (b q) -> p b q", q=QT)
                dve.wait_ge(mask_in, 16)
                step.step(nc.vector.tensor_reduce(has[:, :], mask8[:, :].rearrange("p (t j) -> p t j", j=P), AX_X, ALU.max))
                step.step(nc.vector.tensor_copy(seen4[:, :, 0], has4[:, :, 0]))
                for q in range(1, QT):
                    step.step(nc.vector.tensor_tensor(seen4[:, :, q], seen4[:, :, q - 1], has4[:, :, q], ALU.max))
                pair5 = seen_pair[:, :, :].rearrange("p (b q) k -> p b q k", q=QT)
                for q in range(QT):
                    step.step(nc.vector.tensor_tensor(pair5[:, :, q, :], has4,
                                                      tri[:, q, :].unsqueeze(1).to_broadcast([P, B, QT]), ALU.mult))
                pairs = seen_pair[:, :, :].rearrange("p t k -> p (t k)")
                step.inc(nc.vector.tensor_copy(keep["seen"][:, :], seen[:, :]))
                step.step(nc.vector.tensor_tensor_scan(rank_k[:, :], pairs, zero[:, :], 1.0, ALU.add, ALU.add))
                ranks = rank_k[:, :].rearrange("p (t k) -> p t k", k=QT)
                step.step(nc.vector.tensor_reduce(begin[:, :], seen_pair[:, :, :], AX_X, ALU.add))
                step.step(nc.vector.tensor_tensor(begin[:, :], ranks[:, :, QT - 1], begin[:, :], ALU.subtract))
                step.step(nc.vector.tensor_tensor(carry[:, :].rearrange("p (t k) -> p t k", k=QT), ranks,
                                                  spread(begin[:, :], [P, NT, QT]), ALU.subtract))
                step.inc(nc.vector.tensor_scalar(carry[:, :], carry[:, :], 1.0, None, ALU.is_gt))
                dve.wait_ge(iotas_done, 4)
                dve.wait_ge(slots_done, 1)
                step.inc(nc.vector.tensor_scalar(first[:, :], slot[:, 0:1], 2.0, float(NONE), ALU.is_lt, ALU.mult))
                step.inc(nc.vector.tensor_scalar(diag[:, :], off_diag[:, :], 0.0, None, ALU.is_equal))
                for a in range(2):
                    step.step(nc.vector.scalar_tensor_tensor(hit_k[:, a, :], rank_k[:, :], slot[:, a:a + 1], pairs,
                                                             ALU.is_equal, ALU.mult))
                for a in range(2):
                    for c, column in ((0, key_tile), (2, bias_tile), (3, diag), (4, query_tile), (6, carry)):
                        step.step(nc.vector.scalar_tensor_tensor(junk[:, :], hit_k[:, a, :], 1.0, column[:, :],
                                                                 ALU.mult, ALU.mult, accum_out=kl[:, a, c:c + 1]))
                    step.step(nc.vector.memset(kl[:, a, 7:8], 0.0))
                step.inc(nc.vector.tensor_copy(kl[:, 1, 1:2], kl[:, 1, 0:1]))
                step.inc(nc.vector.tensor_copy(kl[:, 1, 5:6], kl[:, 1, 4:5]))
                step.inc(nc.vector.tensor_tensor(kl[:, 0, 1:2], first[:, :], kl[:, 0, 0:1], ALU.add))
                step.inc(nc.vector.tensor_tensor(kl[:, 0, 5:6], first[:, :], kl[:, 0, 4:5], ALU.add))
                step.step(nc.vector.tensor_copy(kl[:, 0, 7:8], rank_k[:, NT * QT - 1:NT * QT]))
                nc.vector.tensor_copy(kl_i[:, :, :], kl[:, :, :]).then_inc(lists_done, 1)
                for n, (raw, hi, lo) in enumerate(splits):
                    dve.wait_ge(hi_done, n + 1)
                    step.inc(nc.vector.tensor_tensor(lo[:], raw[:], f32(hi[:]), ALU.subtract))
                step.wait()


def matmul3(nc, out, left, right, first, last):
    (lh, ll), (rh, rl) = left, right
    nc.tensor.matmul(out, lh, rh, start=first, stop=False)
    nc.tensor.matmul(out, lh, rl, start=False, stop=False)
    return nc.tensor.matmul(out, ll, rh, start=False, stop=last)


def attend(nc, ctx, io, keep):
    with ExitStack() as scope:
        def sb(name, shape, dt=F32):
            return scope.enter_context(nc.sbuf_tensor("attend_" + name, shape, dt))

        counted = []

        def sem(name):
            counted.append(ctx.enter_context(nc.semaphore("attend_" + name)))
            return counted[-1]

        def bank(name):
            return scope.enter_context(nc.psum_tensor("attend_" + name, [P, 512], F32))

        k_x = sb("k_x", [P, D])
        k_n = sb("k_n", [P, D])
        kx_hi = sb("kx_hi", [P, KD, P], F32R)
        kx_lo = sb("kx_lo", [P, KD, P], F32R)
        kT_hi = sb("kT_hi", [P, 2, P], F32R)
        kT_lo = sb("kT_lo", [P, 2, P], F32R)
        q_x = sb("q_x", [P, D])
        q_n = sb("q_n", [P, D])
        qx_hi = sb("qx_hi", [P, KD, P], F32R)
        qx_lo = sb("qx_lo", [P, KD, P], F32R)
        q = sb("q", [P, H, DH])
        q_null = sb("q_null", [P, H, DH])
        null_dot = sb("null_dot", [P, H])
        qT_hi = sb("qT_hi", [P, KO, P], F32R)
        qT_lo = sb("qT_lo", [P, KO, P], F32R)
        bias_raw = sb("bias_raw", [P, H, P])
        bias = sb("bias", [P, H, P])
        hide = sb("hide", [P, P])
        sc = sb("sc", [P, H, P])
        pT_hi = sb("pT_hi", [P, 2, GH, P], F32R)
        pT_lo = sb("pT_lo", [P, 2, GH, P], F32R)
        neg_max = sb("neg_max", [P, 2, H])
        neg_new = sb("neg_new", [P, H])
        neg_tile = sb("neg_tile", [P, H])
        drop = sb("drop", [P, H])
        alpha = sb("alpha", [P, H])
        acc = sb("acc", [P, 2, H, VW])
        inv_sum = sb("inv_sum", [P, H])
        o = sb("o", [P, H, DH])
        oT_hi = sb("oT_hi", [P, KO, P], F32R)
        oT_lo = sb("oT_lo", [P, KO, P], F32R)
        y = sb("y", [P, D])
        y_sq = sb("y_sq", [P, D], BF16)
        xn = sb("xn", [P, D])
        xnT = sb("xnT", [P, KD, P])
        k_st, k_mv, k_r = sb("k_st", [P, 6]), sb("k_mv", [P, 2]), sb("k_r", [P, 1])
        q_st, q_mv, q_r = sb("q_st", [P, 6]), sb("q_mv", [P, 2]), sb("q_r", [P, 1])
        o_st, o_mv, o_r = sb("o_st", [P, 6]), sb("o_mv", [P, 2]), sb("o_r", [P, 1])
        y_ms, y_r = sb("y_ms", [P, 1]), sb("y_r", [P, 1])

        b_s = [bank("b_s0"), bank("b_s1")]
        b_pT, b_pv, b_4, b_5, b_6, b_7 = (bank(n) for n in ("b_pT", "b_pv", "b_4", "b_5", "b_6", "b_7"))
        b_oT = [b_4, b_6]
        b_xnT = b_logit = b_4
        b_kx = b_kv = b_5
        b_o = b_6
        b_qx = b_7
        b_q = [b_7, b_6]
        b_pT = [b_pT, b_s[0]]
        b_pv = [b_s[1], b_pv]

        k_in, q_in, xn_out = sem("k_in"), sem("q_in"), sem("xn_out")
        bias_in = [sem(f"bias_in{c}") for c in range(NG)]
        k_stats, k_rstd, k_normed, kx_ready, kx_hi_ready, kx_lo_ready = (
            sem(n) for n in ("k_stats", "k_rstd", "k_normed", "kx_ready", "kx_hi_ready", "kx_lo_ready"))
        kv_ready, kT_hi_ready, v_hi_ready, kT_ready, v_ready = (
            sem(n) for n in ("kv_ready", "kT_hi_ready", "v_hi_ready", "kT_ready", "v_ready"))
        bias_ready, scores_ready, scores_biased, max_ready, alpha_ready, probs_ready = (
            sem(n) for n in ("bias_ready", "scores_ready", "scores_biased", "max_ready", "alpha_ready", "probs_ready"))
        pT_ready, pT_hi_ready, pT_lo_ready, pv_ready, acc_ready = (
            sem(n) for n in ("pT_ready", "pT_hi_ready", "pT_lo_ready", "pv_ready", "acc_ready"))
        q_stats, q_rstd, q_normed, qx_ready, qx_hi_ready, qx_lo_ready = (
            sem(n) for n in ("q_stats", "q_rstd", "q_normed", "qx_ready", "qx_hi_ready", "qx_lo_ready"))
        q_ready, q_kept, q_turned, qT_hi_ready, qT_ready, null_ready, max_begun = (
            sem(n) for n in ("q_ready", "q_kept", "q_turned", "qT_hi_ready", "qT_ready", "null_ready", "max_begun"))
        o_ready, oT_ready, oT_hi_ready, oT_lo_ready, proj_ready, o_stats, o_rstd = (
            sem(n) for n in ("o_ready", "oT_ready", "oT_hi_ready", "oT_lo_ready", "proj_ready", "o_stats", "o_rstd"))
        y_ready, y_squared, y_rrms, xn_ready, xnT_ready, xnT_copied, logit_ready, logits_kept = (
            sem(n) for n in ("y_ready", "y_squared", "y_rrms", "xn_ready", "xnT_ready", "xnT_copied",
                             "logit_ready", "logits_kept"))
        v_key, v_pair, v_query, v_out, v_null = (
            sem(n) for n in ("v_key", "v_pair", "v_query", "v_out", "v_null"))
        g_key, g_hide, g_query, g_out, g_rms = (
            sem("g_key"), sem("g_hide"), sem("g_query"), sem("g_out"), sem("g_rms"))
        q_scaled, k_scaled = sem("q_scaled"), sem("k_scaled")
        begun, passed = sem("begun"), sem("passed")
        V_KEY, V_PAIR, V_QUERY, V_OUT = 1, 2 * NG + 2, 1, 2

        ident, half = keep["ident"], keep["half"]

        def number(eng, row, column, most, least=0):
            return eng.value_load(keep["kl"][0:1, bass.ds(row * KCOLS + column, 1)], min_val=least, max_val=most)

        def pairs(eng):
            return number(eng, 0, 7, NPAIR - 4, 1)

        with nc.Block() as block:
            @block.sync
            def _(sp):
                for s in counted:
                    sp.sem_inc(s, 1)

        with nc.Block() as block:
            @block.sync
            def _(sp):
                def load_key(n):
                    at = number(sp, n + 1, 0, NT - 1)
                    sp.dma_start(k_x[:, :], io["x"][bass.ds(at * P, P), :]).then_inc(k_in, 16)

                def load_query(n):
                    at = number(sp, n + 1, 4, NT - 1)
                    sp.dma_start(q_x[:, :], io["x"][bass.ds(at * P, P), :]).then_inc(q_in, 16)

                def load_bias(n, at, c):
                    sp.wait_ge(bias_ready, 1 + n * NG + c - NG + 1)
                    load_bias_now(at, c)

                def load_bias_now(at, c):
                    sp.dma_start(bias_raw[:, c * GH:(c + 1) * GH, :],
                                 io["bias"][bass.ds(at * P, P), c * GH * P:(c + 1) * GH * P]
                                 .rearrange("p (h j) -> p h j", h=GH)).then_inc(bias_in[c], 16)

                def store(n):
                    at = number(sp, n, 5, NT)
                    sp.wait_ge(keep["xn_filled"], 16)
                    sp.wait_ge(xn_ready, 1 + n + 1)
                    sp.dma_start(keep["xn_dram"][bass.ds(at * P, P), :], xn[:, :]).then_inc(xn_out, 16)

                load_query(0)
                load_key(0)
                at = number(sp, 1, 2, QT * QT - 1)
                for c in range(NG):
                    load_bias_now(at, c)
                sp.wait_ge(q_normed, 2)
                load_query(1)
                sp.wait_ge(k_normed, 2)
                load_key(1)
                at = number(sp, 2, 2, QT * QT - 1)
                for c in range(NG):
                    load_bias(1, at, c)
                sp.wait_ge(q_normed, 1 + 2)
                load_query(2)
                sp.wait_ge(k_normed, 1 + 2)
                load_key(2)
                sp.dma_start(keep["xn_dram"][0:N, :].rearrange("(t p) d -> p t d", p=P),
                             keep["g_in"][:, :].unsqueeze(1).to_broadcast([P, NT, D])).then_inc(keep["xn_filled"], 16)
                with sp.Fori(0, pairs(sp)) as i:
                    at = number(sp, i + 3, 2, QT * QT - 1)
                    load_bias(i + 2, at, 0)
                    load_bias(i + 2, at, 1)
                    load_bias(i + 2, at, 2)
                    load_bias(i + 2, at, 3)
                    store(i)
                    sp.wait_ge(q_normed, 1 + i + 3)
                    load_query(i + 3)
                    sp.wait_ge(k_normed, 1 + i + 3)
                    load_key(i + 3)
                n = pairs(sp)
                store(n)
                sp.wait_ge(xn_out, 1 + (n + 1) * 16)
                sp.wait_ge(q_in, 1 + (n + 3) * 16)
                sp.wait_ge(k_in, 1 + (n + 3) * 16)
                for c in range(NG):
                    sp.wait_ge(bias_in[c], 1 + (n + 2) * 16)
                alone(sp, passed)

            @block.gpsimd
            def _(pool):
                def root(n, variance, scale, out, ready, steps, done):
                    pool.wait_ge(ready, 1 + n + 1)
                    alone(pool, passed)
                    nc.gpsimd.tensor_scalar(out, variance, scale, EPS, ALU.mult, ALU.add).then_inc(steps, 1)
                    pool.wait_ge(steps, 1 + n + 1)
                    nc.gpsimd.tensor_tensor(out, out, half[:, :], ALU.pow).then_inc(done, 1)

                def key_root(n):
                    root(n, k_mv[:, 1:2], 1.0, k_r[:, :], k_stats, g_key, k_rstd)

                def query_root(n):
                    root(n, q_mv[:, 1:2], 1.0, q_r[:, :], q_stats, g_query, q_rstd)

                def out_root(n):
                    root(n, o_mv[:, 1:2], 1.0, o_r[:, :], o_stats, g_out, o_rstd)

                def rms_root(n):
                    root(n, y_ms[:, :], 1.0 / D, y_r[:, :], y_squared, g_rms, y_rrms)

                def mask_tile(n):
                    kt = number(pool, n + 1, 1, NT)
                    dg = number(pool, n + 1, 3, 1)
                    pool.wait_ge(bias_ready, 1 + n * NG)
                    nc.gpsimd.tensor_tensor(hide[:, :], keep["hidden"][:, bass.ds(kt, 1), :].rearrange("p o j -> p (o j)"),
                                            keep["causal"][:, bass.ds(dg, 1), :].rearrange("p o j -> p (o j)"),
                                            ALU.add).then_inc(g_hide, 1)
                    pool.wait_ge(g_hide, 1 + n + 1)

                def bias_group(n, c):
                    g = slice(c * GH, (c + 1) * GH)
                    pool.wait_ge(bias_in[c], 1 + (n + 1) * 16)
                    nc.gpsimd.tensor_tensor(bias[:, g, :], bias_raw[:, g, :],
                                            hide[:, :].unsqueeze(1).to_broadcast([P, GH, P]),
                                            ALU.add).then_inc(bias_ready, 1)

                def gain(n, rows, scaled, done):
                    pool.wait_ge(scaled, 1 + n + 1)
                    nc.gpsimd.tensor_tensor(rows[:, :], rows[:, :], keep["g_in"][:, :], ALU.mult).then_inc(done, 1)

                def null_products(n):
                    pool.wait_ge(q_kept, 1 + 2 * n + 2)
                    nc.gpsimd.tensor_tensor(q_null[:, :, :], q[:, :, :],
                                            keep["null_k"][:, :].unsqueeze(1).to_broadcast([P, H, DH]),
                                            ALU.mult).then_inc(null_ready, 1)

                query_root(0)
                gain(0, q_n, q_scaled, q_normed)
                key_root(0)
                gain(0, k_n, k_scaled, k_normed)
                mask_tile(0)
                for c in range(NG):
                    bias_group(0, c)
                query_root(1)
                gain(1, q_n, q_scaled, q_normed)
                key_root(1)
                gain(1, k_n, k_scaled, k_normed)
                null_products(0)

                def next_bias(i, c):
                    pool.wait_ge(scores_biased, 1 + i * NG + c + 1)
                    bias_group(i + 1, c)

                with pool.Fori(0, pairs(pool)) as i:
                    mask_tile(i + 1)
                    for c in range(NG):
                        next_bias(i, c)
                    out_root(i)
                    query_root(i + 2)
                    key_root(i + 2)
                    gain(i + 2, q_n, q_scaled, q_normed)
                    rms_root(i)
                    null_products(i + 1)
                    gain(i + 2, k_n, k_scaled, k_normed)
                n = pairs(pool)
                out_root(n)
                rms_root(n)

            @block.scalar
            def _(act):
                def part(out, source, ready, count, done):
                    act.wait_ge(ready, 1 + count)
                    nc.scalar.activation(out, source, ACT.Copy).then_inc(done, 1)

                def key_rows(n):
                    part(kx_hi[:, :, :], b_kx[:, :].rearrange("p (k t) -> p k t", k=KD), kx_ready, n + 1, kx_hi_ready)

                def key_parts(n):
                    for a in range(2):
                        rows = slice(a * DH, (a + 1) * DH)
                        part(kT_hi[rows, a, :], b_kv[rows, 0:P], kv_ready, n + 1, kT_hi_ready)

                def value_parts(n):
                    act.wait_ge(kT_ready, 1 + 2 * n + 2)
                    part(keep["v_hi"][:, 0:DH], b_kv[:, P:P + DH], kv_ready, n + 1, v_hi_ready)

                def query_rows(n):
                    part(qx_hi[:, :, :], b_qx[:, :].rearrange("p (k t) -> p k t", k=KD), qx_ready, n + 1, qx_hi_ready)

                def query_parts(n, turn):
                    a = turn
                    part(qT_hi[:, 4 * a:4 * a + 4, :], b_q[a][:, :].rearrange("p (g t) -> p g t", g=4),
                         q_turned, 2 * n + turn + 1, qT_hi_ready)

                def keep_queries(n, turn):
                    a = turn
                    act.wait_ge(max_begun, 1 + n)
                    part(q[:, 8 * a:8 * a + 8, :], b_q[a][:, :].rearrange("p (h d) -> p h d", d=DH),
                         q_ready, 2 * n + turn + 1, q_kept)

                def out_parts(n, a):
                    part(oT_hi[:, 4 * a:4 * a + 4, :], b_oT[a][:, :].rearrange("p (g t) -> p g t", g=4),
                         oT_ready, 2 * n + a + 1, oT_hi_ready)

                def square(n):
                    act.wait_ge(y_ready, 1 + n + 1)
                    nc.scalar.activation(y_sq[:, :], y[:, :], ACT.Square, accum_out=y_ms[:, :]).then_inc(y_squared, 1)

                def xn_rows(n):
                    part(xnT[:, :, :], b_xnT[:, :].rearrange("p (k t) -> p k t", k=KD), xnT_ready, n + 1, xnT_copied)

                query_rows(0)
                key_rows(0)
                keep_queries(0, 0)
                keep_queries(0, 1)
                key_parts(0)
                query_parts(0, 0)
                query_parts(0, 1)
                value_parts(0)

                with act.Fori(0, pairs(act)) as i:
                    def probs(c):
                        act.wait_ge(max_ready, 1 + i * NG + c + 1)
                        for h in range(c * GH, (c + 1) * GH):
                            last = nc.scalar.activation(sc[:, h, :], sc[:, h, :], ACT.Exp, bias=neg_new[:, h:h + 1])
                        last.then_inc(probs_ready, 1)
                        nc.scalar.activation(alpha[:, c * GH:(c + 1) * GH], drop[:, c * GH:(c + 1) * GH], ACT.Exp)\
                            .then_inc(alpha_ready, 1)

                    def probs_part(c):
                        part(pT_hi[:, c % 2, :, :], b_pT[c % 2][:, :].rearrange("p (h t) -> p h t", h=GH),
                             pT_ready, i * NG + c + 1, pT_hi_ready)

                    query_rows(i + 1)
                    key_rows(i + 1)
                    out_parts(i, 0)
                    out_parts(i, 1)
                    probs(0)
                    probs(1)
                    keep_queries(i + 1, 0)
                    probs(2)
                    probs(3)
                    probs_part(0)
                    query_parts(i + 1, 0)
                    probs_part(1)
                    key_parts(i + 1)
                    probs_part(2)
                    square(i)
                    probs_part(3)
                    keep_queries(i + 1, 1)
                    query_parts(i + 1, 1)
                    xn_rows(i)
                    act.wait_ge(pv_ready, 1 + (i + 1) * NG)
                    value_parts(i + 1)
                n = pairs(act)
                out_parts(n, 0)
                out_parts(n, 1)
                square(n)
                xn_rows(n)

            @block.vector
            def _(dve):
                def rest(out, source, hi, ready, count, done):
                    dve.wait_ge(ready, 1 + count)
                    nc.vector.tensor_tensor(out, source, f32(hi), ALU.subtract).then_inc(done, 1)

                def stats(n, source, st, mv, steps, per, done):
                    step = Count(dve, steps, 1 + n * per)
                    step.step(nc.vector.bn_stats(st[:, :], source))
                    alone(dve, passed)
                    nc.vector.bn_aggr(mv[:, :], st[:, :]).then_inc(done, 1)

                def norm(n, out, source, mv, r, gain, steps, per, done):
                    step = Count(dve, steps, 1 + n * per + 1)
                    step.step(nc.vector.tensor_scalar(out, source, mv[:, 0:1], r[:, :], ALU.subtract, ALU.mult))
                    nc.vector.tensor_tensor(out, out, gain[:, :], ALU.mult).then_inc(done, 1)

                def key_stats(n):
                    dve.wait_ge(k_in, 1 + (n + 1) * 16)
                    stats(n, k_x[:, :], k_st, k_mv, v_key, V_KEY, k_stats)

                def key_norm(n):
                    dve.wait_ge(k_rstd, 1 + n + 1)
                    dve.wait_ge(kx_ready, 1 + n)
                    nc.vector.tensor_scalar(k_n[:, :], k_x[:, :], k_mv[:, 0:1], k_r[:, :], ALU.subtract, ALU.mult)\
                        .then_inc(k_scaled, 1)

                def key_rows(n):
                    rest(kx_lo[:, :, :], b_kx[:, :].rearrange("p (k t) -> p k t", k=KD), kx_hi[:, :, :],
                         kx_hi_ready, n + 1, kx_lo_ready)

                def key_parts(n):
                    for a in range(2):
                        rows = slice(a * DH, (a + 1) * DH)
                        rest(kT_lo[rows, a, :], b_kv[rows, 0:P], kT_hi[rows, a, :], kT_hi_ready, 2 * n + 2, kT_ready)

                def value_parts(n):
                    rest(keep["v_lo"][:, 0:DH], b_kv[:, P:P + DH], keep["v_hi"][:, 0:DH], v_hi_ready, n + 1, v_ready)

                def query_stats(n):
                    dve.wait_ge(q_in, 1 + (n + 1) * 16)
                    stats(n, q_x[:, :], q_st, q_mv, v_query, V_QUERY, q_stats)

                def query_norm(n):
                    dve.wait_ge(q_rstd, 1 + n + 1)
                    dve.wait_ge(qx_ready, 1 + n)
                    nc.vector.tensor_scalar(q_n[:, :], q_x[:, :], q_mv[:, 0:1], q_r[:, :], ALU.subtract, ALU.mult)\
                        .then_inc(q_scaled, 1)

                def query_rows(n):
                    rest(qx_lo[:, :, :], b_qx[:, :].rearrange("p (k t) -> p k t", k=KD), qx_hi[:, :, :],
                         qx_hi_ready, n + 1, qx_lo_ready)

                def query_parts(n, turn):
                    a = turn
                    rest(qT_lo[:, 4 * a:4 * a + 4, :], b_q[a][:, :].rearrange("p (g t) -> p g t", g=4),
                         qT_hi[:, 4 * a:4 * a + 4, :], qT_hi_ready, 2 * n + turn + 1, qT_ready)

                def begin_max(n):
                    step = Count(dve, v_null, 1 + n)
                    dve.wait_ge(null_ready, 1 + n + 1)
                    step.step(nc.vector.tensor_reduce(null_dot[:, :], q_null[:, :, :], AX_X, ALU.add))
                    nc.vector.scalar_tensor_tensor(neg_max[:, 0, :], null_dot[:, :], -SCALE, keep["null_bias"][:, :],
                                                   ALU.mult, ALU.add).then_inc(max_begun, 1)

                def out_parts(n, a):
                    rest(oT_lo[:, 4 * a:4 * a + 4, :], b_oT[a][:, :].rearrange("p (g t) -> p g t", g=4),
                         oT_hi[:, 4 * a:4 * a + 4, :], oT_hi_ready, 2 * n + a + 1, oT_lo_ready)

                def out_stats(n):
                    dve.wait_ge(proj_ready, 1 + n + 1)
                    stats(n, b_o[:, :], o_st, o_mv, v_out, V_OUT, o_stats)

                def out_norm(n):
                    dve.wait_ge(o_rstd, 1 + n + 1)
                    norm(n, y[:, :], b_o[:, :], o_mv, o_r, keep["g_out"], v_out, V_OUT, y_ready)

                def out_rows(n):
                    dve.wait_ge(y_rrms, 1 + n + 1)
                    dve.wait_ge(xn_out, 1 + n * 16)
                    nc.vector.scalar_tensor_tensor(xn[:, :], y[:, :], y_r[:, :], keep["norm_w"][:, :],
                                                   ALU.mult, ALU.mult).then_inc(xn_ready, 1)

                def keep_logits(n, at):
                    dve.wait_ge(logit_ready, 1 + n + 1)
                    nc.vector.tensor_tensor(keep["logits"][:, bass.ds(at, 1), :].rearrange("p o e -> p (o e)"),
                                            b_logit[:, 0:E], keep["router_b"][:, :], ALU.add).then_inc(logits_kept, 1)

                def prepare(n):
                    query_stats(n)
                    query_norm(n)
                    key_stats(n)
                    key_norm(n)

                prepare(0)
                query_rows(0)
                key_rows(0)
                nc.vector.tensor_copy(acc[:, 0, :, :], keep["null_v"][:, :].unsqueeze(1).to_broadcast([P, H, VW]))\
                    .then_inc(begun, 1)
                nc.vector.memset(acc[:, 1, :, :], 0.0).then_inc(begun, 1)
                nc.vector.memset(neg_max[:, 1, :], 0.0).then_inc(begun, 1)
                nc.vector.memset(o[:, :, :], 0.0).then_inc(o_ready, 1)
                for parts in (kT_hi, kT_lo):
                    for a in range(2):
                        nc.vector.memset(f32(parts[a * DH:(a + 1) * DH, 1 - a, :]), 0.0).then_inc(begun, 1)
                dve.wait_ge(begun, 1 + 7)
                key_parts(0)
                query_parts(0, 0)
                query_parts(0, 1)
                prepare(1)
                value_parts(0)

                with dve.Fori(0, pairs(dve)) as i:
                    step = Count(dve, v_pair, 1 + i * V_PAIR)

                    def biased(c):
                        g = slice(c * GH, (c + 1) * GH)
                        dve.wait_ge(bias_ready, 1 + i * NG + c + 1)
                        dve.wait_ge(scores_ready, 1 + i * NG + c + 1)
                        nc.vector.scalar_tensor_tensor(sc[:, g, :], b_s[c % 2][:, :].rearrange("p (h t) -> p h t", h=GH),
                                                       SCALE, bias[:, g, :], ALU.mult, ALU.add).then_inc(scores_biased, 1)

                    def highest(c):
                        g = slice(c * GH, (c + 1) * GH)
                        dve.wait_ge(scores_biased, 1 + i * NG + c + 1)
                        step.step(nc.vector.tensor_reduce(neg_tile[:, g], sc[:, g, :], AX_X, ALU.max, negate=True))

                    def raised(c):
                        g = slice(c * GH, (c + 1) * GH)
                        before = neg_max[:, bass.ds(carry, 1), g].rearrange("p o h -> p (o h)")
                        step.step(nc.vector.tensor_tensor(neg_new[:, g], before, neg_tile[:, g], ALU.min))
                        nc.vector.tensor_tensor(drop[:, g], neg_new[:, g], before, ALU.subtract).then_inc(max_ready, 1)

                    def scores(c):
                        biased(c)
                        highest(c)
                        raised(c)

                    def probs_part(c):
                        rest(pT_lo[:, c % 2, :, :], b_pT[c % 2][:, :].rearrange("p (h t) -> p h t", h=GH),
                             pT_hi[:, c % 2, :, :],
                             pT_hi_ready, i * NG + c + 1, pT_lo_ready)

                    def accumulate(c):
                        dve.wait_ge(alpha_ready, 1 + i * NG + c + 1)
                        dve.wait_ge(pv_ready, 1 + i * NG + c + 1)
                        for n in range(GH):
                            h = c * GH + n
                            last = nc.vector.scalar_tensor_tensor(
                                acc[:, 1, h, :], acc[:, bass.ds(carry, 1), h, :].rearrange("p o d -> p (o d)"),
                                alpha[:, h:h + 1], b_pv[c % 2][:, n * VW:(n + 1) * VW], ALU.mult, ALU.add)
                        last.then_inc(acc_ready, 1)

                    biased(0)
                    carry = number(dve, i + 1, 6, 1)
                    highest(0)
                    query_rows(i + 1)
                    begin_max(i)
                    dve.wait_ge(max_begun, 1 + i + 1)
                    dve.wait_ge(v_pair, 1 + i * V_PAIR + 1)
                    raised(0)
                    out_parts(i, 0)
                    out_parts(i, 1)
                    scores(1)
                    key_rows(i + 1)
                    scores(2)
                    scores(3)
                    dve.wait_ge(max_ready, 1 + (i + 1) * NG)
                    step.inc(nc.vector.tensor_copy(neg_max[:, 1, :], neg_new[:, :]))
                    out_stats(i)
                    probs_part(0)
                    query_parts(i + 1, 0)
                    probs_part(1)
                    out_norm(i)
                    query_stats(i + 2)
                    key_stats(i + 2)
                    key_parts(i + 1)
                    accumulate(0)
                    probs_part(2)
                    query_norm(i + 2)
                    accumulate(1)
                    probs_part(3)
                    out_rows(i)
                    key_norm(i + 2)
                    at = number(dve, i, 5, NT)
                    accumulate(2)
                    query_parts(i + 1, 1)
                    accumulate(3)
                    value_parts(i + 1)
                    dve.wait_ge(acc_ready, 1 + (i + 1) * NG)
                    step.step(nc.vector.reciprocal(inv_sum[:, :], acc[:, 1, :, DH]))
                    nc.vector.tensor_tensor(o[:, :, :], acc[:, 1, :, 0:DH], spread(inv_sum[:, :], [P, H, DH]), ALU.mult)\
                        .then_inc(o_ready, 1)
                    keep_logits(i, at)
                    assert step.n == V_PAIR
                n = pairs(dve)
                at = number(dve, n, 5, NT)
                out_parts(n, 0)
                out_parts(n, 1)
                out_stats(n)
                out_norm(n)
                out_rows(n)
                keep_logits(n, at)

            @block.tensor
            def _(pe):
                def turn(b, source, n, ready, count, done):
                    pe.wait_ge(ready, 1 + count)
                    for k in range(n):
                        last = nc.tensor.transpose(b[:, k * P:(k + 1) * P], source(k), ident[:, :])
                    last.then_inc(done, 1)

                def key_rows(n):
                    pe.wait_ge(v_ready, 1 + n)
                    turn(b_kx, lambda k: k_n[:, k * P:(k + 1) * P], KD, k_normed, n + 1, kx_ready)

                def keys_values(n):
                    pe.wait_ge(kx_lo_ready, 1 + n + 1)
                    hi, lo = keep["wkv_hi"], keep["wkv_lo"]
                    for k in range(KD):
                        matmul3(nc, b_kv[:, 0:P], (hi[:, k, 0:P], lo[:, k, 0:P]), (kx_hi[:, k, :], kx_lo[:, k, :]),
                                k == 0, k == KD - 1)
                    for k in range(KD):
                        last = matmul3(nc, b_kv[:, P:P + DH], (kx_hi[:, k, :], kx_lo[:, k, :]),
                                       (hi[:, k, P:P + DH], lo[:, k, P:P + DH]), k == 0, k == KD - 1)
                    last.then_inc(kv_ready, 1)

                def query_rows(n):
                    pe.wait_ge(qT_ready, 1 + 2 * n)
                    turn(b_qx, lambda k: q_n[:, k * P:(k + 1) * P], KD, q_normed, n + 1, qx_ready)

                def queries(n, turn):
                    pe.wait_ge(qx_lo_ready, 1 + n + 1)
                    a = turn
                    cols = slice(a * 512, (a + 1) * 512)
                    for k in range(KD):
                        last = matmul3(nc, b_q[a][:, :], (qx_hi[:, k, :], qx_lo[:, k, :]),
                                       (keep["wq_hi"][:, k, cols], keep["wq_lo"][:, k, cols]), k == 0, k == KD - 1)
                    last.then_inc(q_ready, 1)

                def queries_turned(n, t):
                    a = t
                    turn(b_q[a], lambda k: q[:, :, :].rearrange("p h d -> p (h d)")
                         [:, (4 * a + k) * P:(4 * a + k + 1) * P], 4, q_kept, 2 * n + t + 1, q_turned)

                def out_turned(n):
                    pe.wait_ge(logits_kept, 1 + n)
                    pe.wait_ge(qT_ready, 1 + 2 * n + 2)
                    for a in range(2):
                        turn(b_oT[a], lambda k, a=a: o[:, :, :].rearrange("p h d -> p (h d)")
                             [:, (4 * a + k) * P:(4 * a + k + 1) * P], 4, o_ready, n + 1, oT_ready)

                def project(n):
                    pe.wait_ge(oT_lo_ready, 1 + 2 * n + 2)
                    for k in range(KO):
                        last = matmul3(nc, b_o[:, :], (oT_hi[:, k, :], oT_lo[:, k, :]),
                                       (keep["wo_hi"][:, k, :], keep["wo_lo"][:, k, :]), k == 0, k == KO - 1)
                    last.then_inc(proj_ready, 1)

                def xn_turned(n):
                    turn(b_xnT, lambda k: xn[:, k * P:(k + 1) * P], KD, xn_ready, n + 1, xnT_ready)

                def logits(n):
                    pe.wait_ge(xnT_copied, 1 + n + 1)
                    for k in range(KD):
                        last = nc.tensor.matmul(b_logit[:, 0:E], xnT[:, k, :], keep["router_wT"][:, k, :],
                                                start=(k == 0), stop=(k == KD - 1))
                    last.then_inc(logit_ready, 1)

                query_rows(0)
                key_rows(0)
                queries(0, 0)
                queries(0, 1)
                keys_values(0)
                queries_turned(0, 0)
                queries_turned(0, 1)

                with pe.Fori(0, pairs(pe)) as i:
                    def scores(c):
                        if c >= 2:
                            pe.wait_ge(scores_biased, 1 + i * NG + c - 1)
                        for n in range(GH // 2):
                            g = c * GH // 2 + n
                            last = matmul3(nc, b_s[c % 2][:, 2 * n * P:2 * (n + 1) * P], (qT_hi[:, g, :], qT_lo[:, g, :]),
                                           (kT_hi[:, :, :].rearrange("p a t -> p (a t)"),
                                            kT_lo[:, :, :].rearrange("p a t -> p (a t)")), True, True)
                        last.then_inc(scores_ready, 1)

                    def turned(c):
                        if c == 1:
                            pe.wait_ge(scores_biased, 1 + i * NG + NG)
                        elif c >= 2:
                            pe.wait_ge(pT_lo_ready, 1 + i * NG + c - 1)
                        turn(b_pT[c % 2], lambda k: sc[:, c * GH + k, :], GH, probs_ready, i * NG + c + 1, pT_ready)

                    def products(c):
                        pe.wait_ge(pT_lo_ready, 1 + i * NG + c + 1)
                        if c == 0:
                            pe.wait_ge(scores_biased, 1 + i * NG + NG)
                        if c >= 2:
                            pe.wait_ge(acc_ready, 1 + i * NG + c - 1)
                        for n in range(GH):
                            last = matmul3(nc, b_pv[c % 2][:, n * VW:(n + 1) * VW],
                                           (pT_hi[:, c % 2, n, :], pT_lo[:, c % 2, n, :]),
                                           (keep["v_hi"][:, :], keep["v_lo"][:, :]), True, True)
                        last.then_inc(pv_ready, 1)

                    pe.wait_ge(kT_ready, 1 + 2 * i + 2)
                    pe.wait_ge(qT_ready, 1 + 2 * i + 1)
                    scores(0)
                    pe.wait_ge(acc_ready, 1 + i * NG)
                    scores(1)
                    query_rows(i + 1)
                    key_rows(i + 1)
                    pe.wait_ge(qT_ready, 1 + 2 * i + 2)
                    out_turned(i)
                    scores(2)
                    queries(i + 1, 0)
                    scores(3)
                    project(i)
                    turned(0)
                    queries_turned(i + 1, 0)
                    turned(1)
                    keys_values(i + 1)
                    products(0)
                    turned(2)
                    products(1)
                    turned(3)
                    pe.wait_ge(y_ready, 1 + i + 1)
                    queries(i + 1, 1)
                    products(2)
                    queries_turned(i + 1, 1)
                    xn_turned(i)
                    products(3)
                    logits(i)
                n = pairs(pe)
                out_turned(n)
                project(n)
                xn_turned(n)
                logits(n)


def route(nc, ctx, io, keep):
    J = NT // (P // E)
    L = P // E
    W = J * P
    with ExitStack() as scope:
        def sb(name, shape, dt=F32):
            return scope.enter_context(nc.sbuf_tensor("route_" + name, shape, dt))

        def sem(name):
            return ctx.enter_context(nc.semaphore("route_" + name))

        def bank(name):
            return scope.enter_context(nc.psum_tensor("route_" + name, [P, 512], F32))

        lg = sb("lg", [P, J, L, E])
        gate = sb("gate", [P, J, L, E])
        stand_in = sb("stand_in", [P, J, L, E])
        unseen = sb("unseen", [P, NT])
        row_max = sb("row_max", [P, NT])
        row_sum = sb("row_sum", [P, NT])
        val = sb("val", [P, W])
        flag = sb("flag", [P, W])
        greater = sb("greater", [P, W])
        equal = sb("equal", [P, W])
        rank = sb("rank", [P, W])
        zero = sb("zero", [P, W])
        count = sb("count", [P, 1])
        cand = sb("cand", [P, 1], I32)
        undo = sb("undo", [P, 1], I32)
        bit_f = sb("bit_f", [P, 1])
        bit_i = sb("bit_i", [P, 1], I32)
        need = sb("need", [P, 1])
        same_i = sb("same_i", [P, P], I32)
        same = sb("same", [P, P])
        before = sb("before", [P, P])
        taken = sb("taken", [P, J, L, E])
        pos_f = sb("pos_f", [P, EP, NT])
        pos_i = sb("pos_i", [P, EP, NT], I32)
        pos_p = sb("pos_p", [P, EP, NT], I32)
        tile_id = sb("tile_id_r", [P, NT])
        part_id = sb("part_id_r", [P, 1])
        source = sb("source", [P, NT])
        meta = sb("meta", [P, NT, META])
        b_val = [bank("b_val0"), bank("b_val1")]
        b_pos = [bank("b_pos0"), bank("b_pos1")]
        b_cnt, b_gt, b_eq, b_sel = bank("b_cnt"), bank("b_gt"), bank("b_eq"), bank("b_sel")

        lg_ready, val_turned, val_ready = sem("lg_ready"), sem("val_turned"), sem("val_ready")
        iota_ready, same_int, same_ready, before_ready = (
            sem("iota_ready"), sem("same_int"), sem("same_ready"), sem("before_ready"))
        counted, summed, exp_ready, shifted = sem("counted"), sem("summed"), sem("exp_ready"), sem("shifted")
        gt_counted, eq_counted, sel_counted = sem("gt_counted"), sem("eq_counted"), sem("sel_counted")
        gt_summed, eq_summed, sel_summed = sem("gt_summed"), sem("eq_summed"), sem("sel_summed")
        pos_ready, pos_turned, meta_ready, meta_out = (
            sem("pos_ready"), sem("pos_turned"), sem("meta_ready"), sem("meta_out"))
        r_step, r_bit = sem("r_step"), sem("r_bit")
        BITS, UNROLL = 31, 10

        def by_tile(ap):
            return ap.rearrange("p (l j) e -> p j l e", j=J)

        def by_tile1(ap):
            return ap.rearrange("p (l j) -> p j l", j=J)

        def over_experts(ap):
            return by_tile1(ap).unsqueeze(3).to_broadcast([P, J, L, E])

        with nc.Block() as block:
            @block.gpsimd
            def _(pool):
                pool.iota(same_i[:, :], [[1, P]], base=P, channel_multiplier=-1).then_inc(same_int, 1)
                pool.iota(tile_id[:, :], [[1, NT]], base=0, channel_multiplier=0,
                          allow_small_or_imprecise_dtypes=True).then_inc(iota_ready, 1)
                pool.iota(part_id[:, :], [[1, 1]], base=0, channel_multiplier=1,
                          allow_small_or_imprecise_dtypes=True).then_inc(iota_ready, 1)
                pool.iota(keep["ids_a"][:, :], [[1, 16]], base=0, channel_multiplier=0,
                          allow_small_or_imprecise_dtypes=True).then_inc(iota_ready, 1)
                pool.iota(keep["ids_b"][:, :], [[1, 32]], base=0, channel_multiplier=0,
                          allow_small_or_imprecise_dtypes=True).then_inc(iota_ready, 1)
                pool.memset(zero[:, :], 0.0).then_inc(iota_ready, 1)
                pool.memset(meta[:, :, :], 0.0).then_inc(iota_ready, 1)
                pool.memset(pos_f[:, E:EP, :], -1.0).then_inc(iota_ready, 1)
                pool.wait_ge(same_ready, 1)
                pool.affine_select(out=before[:, :], in_=same[:, :], compare_op=ALU.is_gt, fill=0.0, base=0,
                                   pattern=[[1, P]], channel_multiplier=-1).then_inc(before_ready, 1)

            @block.tensor
            def _(pe):
                pe.wait_ge(lg_ready, 1)
                for j in range(J):
                    last = nc.tensor.transpose(b_val[j // 4][:, (j % 4) * P:(j % 4 + 1) * P],
                                               lg[:, j, :, :].rearrange("p l e -> p (l e)"), keep["ident"][:, :])
                last.then_inc(val_turned, 1)
                pe.wait_ge(same_ready, 1)
                with pe.Fori(0, BITS + 1) as i:
                    pe.wait_ge(counted, i + 1)
                    nc.tensor.matmul(b_cnt[:, 0:1], same[:, :], count[:, :], start=True, stop=True).then_inc(summed, 1)
                pe.wait_ge(gt_counted, 1)
                nc.tensor.matmul(b_gt[:, 0:1], same[:, :], count[:, :], start=True, stop=True).then_inc(gt_summed, 1)
                pe.wait_ge(before_ready, 1)
                pe.wait_ge(eq_counted, 1)
                nc.tensor.matmul(b_eq[:, 0:1], before[:, :], rank[:, W - 1:W], start=True, stop=True).then_inc(eq_summed, 1)
                pe.wait_ge(sel_counted, 1)
                nc.tensor.matmul(b_sel[:, 0:1], before[:, :], rank[:, W - 1:W], start=True, stop=True).then_inc(sel_summed, 1)
                pe.wait_ge(pos_ready, 1)
                for j in range(J):
                    last = nc.tensor.transpose(b_pos[j // 4][:, (j % 4) * P:(j % 4 + 1) * P],
                                               flag[:, j * P:(j + 1) * P], keep["ident"][:, :])
                last.then_inc(pos_turned, 1)

            @block.scalar
            def _(act):
                act.wait_ge(val_turned, 1)
                for a in range(2):
                    last = nc.scalar.activation(val[:, a * 512:(a + 1) * 512], b_val[a][:, :], ACT.Copy)
                last.then_inc(val_ready, 1)
                act.wait_ge(shifted, 1)
                nc.scalar.activation(gate[:, :, :, :], gate[:, :, :, :], ACT.Exp).then_inc(exp_ready, 1)

            @block.vector
            def _(dve):
                step = Count(dve, r_step)
                logits = by_tile(keep["logits"][:, 0:NT, :])
                none = keep["logits"][:, NONE, :].unsqueeze(1).unsqueeze(1).to_broadcast([P, J, L, E])
                step.step(nc.vector.tensor_scalar(unseen[:, :], keep["seen"][:, :], -1.0, 1.0, ALU.mult, ALU.add))
                step.inc(nc.vector.tensor_tensor(lg[:, :, :, :], logits, over_experts(keep["seen"][:, :]), ALU.mult))
                step.step(nc.vector.tensor_tensor(stand_in[:, :, :, :], none, over_experts(unseen[:, :]), ALU.mult))
                nc.vector.tensor_tensor(lg[:, :, :, :], lg[:, :, :, :], stand_in[:, :, :, :], ALU.add).then_inc(lg_ready, 1)
                dve.wait_ge(same_int, 1)
                step.step(nc.vector.tensor_scalar(same_i[:, :], same_i[:, :], E - 1, None, ALU.bitwise_and))
                nc.vector.tensor_scalar(same[:, :], same_i[:, :], 0.0, None, ALU.is_equal).then_inc(same_ready, 1)
                dve.wait_ge(lg_ready, 1)
                rows = lg[:, :, :, :].rearrange("p j l e -> p (j l) e")
                gates = gate[:, :, :, :].rearrange("p j l e -> p (j l) e")
                step.step(nc.vector.tensor_reduce(row_max[:, :], rows, AX_X, ALU.max))
                nc.vector.tensor_tensor(gates, rows, spread(row_max[:, :], [P, NT, E]), ALU.subtract).then_inc(shifted, 1)

                def reach(limit):
                    nc.vector.tensor_scalar(flag[:, :], val[:, :], limit, None, ALU.is_ge, ALU.add,
                                            accum_out=count[:, :]).then_inc(counted, 1)

                dve.wait_ge(val_ready, 1)
                reach(0.0)
                step.inc(nc.vector.memset(bit_f[:, :], float(1 << BITS)))
                step.inc(nc.vector.memset(bit_i[:, :], 1 << (BITS - 1)))
                dve.wait_ge(summed, 1)
                step.step(nc.vector.tensor_scalar(undo[:, :], b_cnt[:, 0:1], float(CAP), -1.0, ALU.is_lt, ALU.mult))
                nc.vector.tensor_scalar(cand[:, :], undo[:, :], 1 << (BITS - 1), None, ALU.bitwise_xor)\
                    .then_inc(r_bit, 1)

                def next_bit(i):
                    dve.wait_ge(r_bit, 1 + i * 4)
                    reach(cand[:, :].bitcast(F32))
                    nc.vector.tensor_scalar(bit_f[:, :], bit_f[:, :], 0.5, None, ALU.mult).then_inc(r_bit, 1)
                    nc.vector.tensor_scalar(bit_i[:, :], bit_i[:, :], 1, None, ALU.logical_shift_right).then_inc(r_bit, 1)
                    dve.wait_ge(summed, i + 2)
                    dve.wait_ge(r_bit, 1 + i * 4 + 2)
                    nc.vector.tensor_scalar(undo[:, :], b_cnt[:, 0:1], float(CAP), bit_f[:, :], ALU.is_lt, ALU.mult)\
                        .then_inc(r_bit, 1)
                    dve.wait_ge(r_bit, 1 + i * 4 + 3)
                    nc.vector.scalar_tensor_tensor(cand[:, :], undo[:, :], bit_i[:, :], cand[:, :],
                                                   ALU.bitwise_xor, ALU.bitwise_xor).then_inc(r_bit, 1)

                with dve.Fori(0, BITS // UNROLL) as i:
                    for n in range(UNROLL):
                        next_bit(i * UNROLL + n)
                for n in range(BITS // UNROLL * UNROLL, BITS):
                    next_bit(n)
                dve.wait_ge(r_bit, 1 + BITS * 4)
                limit = cand[:, :].bitcast(F32)

                nc.vector.tensor_scalar(greater[:, :], val[:, :], limit, None, ALU.is_gt, ALU.add,
                                        accum_out=count[:, :]).then_inc(gt_counted, 1)
                step.step(nc.vector.tensor_scalar(equal[:, :], val[:, :], limit, None, ALU.is_equal))
                dve.wait_ge(iota_ready, 7)
                nc.vector.tensor_tensor_scan(rank[:, :], equal[:, :], zero[:, :], 0.0, ALU.add, ALU.add)\
                    .then_inc(eq_counted, 1)
                dve.wait_ge(gt_summed, 1)
                step.step(nc.vector.tensor_scalar(need[:, :], b_gt[:, 0:1], -1.0, float(CAP), ALU.mult, ALU.add))
                dve.wait_ge(eq_summed, 1)
                step.step(nc.vector.tensor_tensor(need[:, :], need[:, :], b_eq[:, 0:1], ALU.subtract))
                step.step(nc.vector.scalar_tensor_tensor(flag[:, :], rank[:, :], need[:, :], equal[:, :],
                                                         ALU.is_le, ALU.mult))
                step.step(nc.vector.tensor_tensor(flag[:, :], flag[:, :], greater[:, :], ALU.add))
                nc.vector.tensor_tensor_scan(rank[:, :], flag[:, :], zero[:, :], 0.0, ALU.add, ALU.add)\
                    .then_inc(sel_counted, 1)
                dve.wait_ge(exp_ready, 1)
                step.step(nc.vector.tensor_reduce(row_sum[:, :], gates, AX_X, ALU.add))
                step.step(nc.vector.reciprocal(row_sum[:, :], row_sum[:, :]))
                step.inc(nc.vector.tensor_tensor(gates, gates, spread(row_sum[:, :], [P, NT, E]), ALU.mult))
                dve.wait_ge(sel_summed, 1)
                nc.vector.scalar_tensor_tensor(flag[:, :], rank[:, :], b_sel[:, 0:1], flag[:, :], ALU.add, ALU.mult)\
                    .then_inc(pos_ready, 1)
                step.step(nc.vector.tensor_scalar(source[:, :], tile_id[:, :], -float(NONE), None, ALU.add))
                step.step(nc.vector.tensor_tensor(source[:, :], source[:, :], keep["seen"][:, :], ALU.mult))
                step.step(nc.vector.tensor_scalar(source[:, :], source[:, :], float(NONE), float(P), ALU.add, ALU.mult))
                step.inc(nc.vector.tensor_scalar(meta[:, :, E].bitcast(I32), source[:, :], part_id[:, :], None, ALU.add))
                dve.wait_ge(pos_turned, 1)
                for a in range(2):
                    turned = b_pos[a][:, :].rearrange("p (j l e) -> p j l e", l=L, e=E)
                    js = slice(a * J // 2, (a + 1) * J // 2)
                    step.inc(nc.vector.tensor_scalar(taken[:, js, :, :], turned, 0.0, None, ALU.is_gt))
                    for j in range(J // 2):
                        out = pos_f[:, 0:E, :].rearrange("p e (l j) -> p j l e", j=J)[:, a * J // 2 + j, :, :]
                        step.inc(nc.vector.tensor_scalar(out, turned[:, j, :, :], -1.0, None, ALU.add))
                step.wait()
                step.step(nc.vector.tensor_tensor(gate[:, :, :, :], gate[:, :, :, :], taken[:, :, :, :], ALU.mult))
                step.step(nc.vector.tensor_reduce(row_sum[:, :], gates, AX_X, ALU.add))
                step.step(nc.vector.tensor_scalar(row_max[:, :], row_sum[:, :], 0.0, None, ALU.is_equal))
                step.step(nc.vector.tensor_tensor(row_sum[:, :], row_sum[:, :], row_max[:, :], ALU.add))
                step.step(nc.vector.reciprocal(row_sum[:, :], row_sum[:, :]))
                nc.vector.tensor_tensor(meta[:, :, 0:E].rearrange("p (l j) e -> p j l e", j=J), gate[:, :, :, :],
                                        row_sum[:, :].rearrange("p (j l) -> p j l", j=J).unsqueeze(3)
                                        .to_broadcast([P, J, L, E]), ALU.mult).then_inc(meta_ready, 1)
                step.step(nc.vector.tensor_copy(pos_i[:, :, :], pos_f[:, :, :]))
                step.step(nc.vector.tensor_scalar(pos_p[:, :, :], pos_i[:, :, :], 5, None, ALU.arith_shift_right))
                step.inc(nc.vector.tensor_copy(keep["pos_a"][:, :, :], pos_p[:, :, :]))
                step.step(nc.vector.tensor_scalar(pos_i[:, :, :], pos_i[:, :, :], 31, None, ALU.bitwise_and))
                step.inc(nc.vector.tensor_copy(keep["pos_b"][:, :, :], pos_i[:, :, :]))
                step.inc(nc.vector.tensor_copy(keep["tile_ids"][:, :], tile_id[:, :]))
                step.inc(nc.vector.tensor_copy(keep["part_id"][:, :], part_id[:, :]))
                step.wait()

            @block.sync
            def _(sp):
                sp.dma_start(io["out"].rearrange("(a n) d -> a (n d)", a=16),
                             io["x"].rearrange("(a n) d -> a (n d)", a=16)).then_inc(keep["x_copied"], 16)
                sp.wait_ge(meta_ready, 1)
                sp.dma_start(keep["meta_dram"].rearrange("(t p) c -> p t c", p=P), meta[:, :, :]).then_inc(meta_out, 16)
                sp.wait_ge(meta_out, 16)


def experts(nc, ctx, io, keep):
    RING = 4
    HB = 2
    with ExitStack() as scope:
        def sb(name, shape, dt=F32):
            return scope.enter_context(nc.sbuf_tensor("experts_" + name, shape, dt))

        def sem(name):
            return ctx.enter_context(nc.semaphore("experts_" + name))

        def bank(name):
            return scope.enter_context(nc.psum_tensor("experts_" + name, [P, 512], F32))

        w_raw = sb("w_raw", [P, RING, 2 * D])
        w_hi = sb("w_hi", [P, RING, 2 * D], F32R)
        w_lo = sb("w_lo", [P, RING, 2 * D], F32R)
        h = sb("h", [P, HB, CAP])
        h_hi = sb("h_hi", [P, HB, CAP], F32R)
        h_lo = sb("h_lo", [P, HB, CAP], F32R)
        b1 = sb("b1_sb", [P, E, FT])
        b2 = sb("b2_sb", [P, E, D])
        hot_a = sb("hot_a", [P, NT, 16], BF16)
        hot_b = sb("hot_b", [P, NT, 32], BF16)
        named = sb("named", [P, NT, 2, 32], BF16)
        list_i = sb("list_i", [16, 32], I32)
        name_f = sb("name_f", [16, 32])
        next_ids = sb("next_ids", [P, CT], U32)
        ids = sb("ids", [P, CT], U32)
        rows_meta = sb("rows_meta", [P, CT, META])
        rows_id = sb("rows_id", [P, CT], U32)
        weight = sb("weight", [P, CT])
        warm = sb("warm", [P, 1])
        rows = sb("rows", [P, CT, D])
        xT_hi = sb("xT_hi", [P, 2, KD, CAP], F32R)
        xT_lo = sb("xT_lo", [P, 2, KD, CAP], F32R)
        bias_w = sb("bias_w", [P, CT, D])
        y = sb("y_out", [P, CT, D])
        b_h = [bank("b_h0"), bank("b_h1")]
        b_y = [bank(f"b_y{c}") for c in range(CT)]
        b_list, b_x = bank("b_list"), bank("b_x")

        w_in = [sem(f"w_in{slot}") for slot in range(RING)]
        w_hi_ready, w_lo_ready = sem("w_hi_ready"), sem("w_lo_ready")
        b1_loaded, b2_loaded = sem("b1_loaded"), sem("b2_loaded")
        h_ready, h_done, h_hi_ready, h_lo_ready = sem("h_ready"), sem("h_done"), sem("h_hi_ready"), sem("h_lo_ready")
        y_ready, y_scaled, y_added = sem("yb_ready"), sem("y_scaled"), sem("y_added")
        hot_ready, list_summed, list_ready, list_moved = (
            sem("hot_ready"), sem("list_summed"), sem("list_ready"), sem("list_moved"))
        meta_in, rows_in, weight_ready, bias_ready = (
            sem("meta_in"), sem("rows_in"), sem("weight_ready"), sem("bias_w_ready"))
        ids_ready, rows_id_ready = sem("ids_ready"), sem("rows_id_ready")
        x_turned, x_hi_ready, x_lo_ready = sem("x_turned"), sem("x_hi_ready"), sem("x_lo_ready")
        f_hot, f_list, passed = sem("f_hot"), sem("f_list"), sem("f_passed")

        HOT, LIST, NAME, TURN = 0, 5, 6, 11

        with nc.Block() as block:
            @block.sync
            def _(sp):
                def load(chunk, slot):
                    sp.dma_start(w_raw[:, slot, :], io["w"][bass.ds(chunk, 1), :, :].rearrange("o p n -> p (o n)"))\
                        .then_inc(w_in[slot], 16)

                sp.dma_start(b1[:, :, :], io["b1"]).then_inc(b1_loaded, 16)
                for g in range(RING):
                    load(g, g)
                sp.wait_ge(rows_in, CT * 16)
                sp.dma_start(b2[:, :, :].rearrange("p e d -> p (e d)"), io["b2"].to_broadcast([P, E * D]))\
                    .then_inc(b2_loaded, 16)
                with sp.Fori(0, E * FT // RING - 1) as i:
                    for g in range(RING):
                        sp.wait_ge(w_lo_ready, i * RING + g + 1)
                        load(i * RING + (RING + g), g)
                for g in range(2):
                    sp.wait_ge(w_lo_ready, E * FT - RING + g + 1)
                    load(g, g)
                for g in range(2):
                    sp.wait_ge(w_in[g], (E * FT // RING + 1) * 16)
                sp.wait_ge(b2_loaded, 16)

            @block.gpsimd
            def _(pool):
                def fetch(n):
                    pool.wait_ge(list_ready, n + 1)
                    alone(pool, passed)
                    pool.dma_start(next_ids[:, :], list_i[:, :].bitcast(U32)).then_inc(list_moved, 16)
                    pool.wait_ge(list_moved, (n + 1) * 16)
                    alone(pool, passed)
                    for c in range(CT):
                        pool.indirect_dma_start(rows_meta[:, c, :], None, keep["meta_dram"],
                                                bass.IndirectOffsetOnAxis(next_ids[:, c:c + 1], 0)).then_inc(meta_in, 16)
                    pool.wait_ge(meta_in, (n + 1) * CT * 16)
                    alone(pool, passed)
                    nc.gpsimd.tensor_copy(rows_id[:, :], rows_meta[:, :, E].bitcast(U32)).then_inc(rows_id_ready, 1)
                    pool.wait_ge(rows_id_ready, n + 1)
                    pool.wait_ge(x_turned, n * KD)
                    alone(pool, passed)
                    for c in range(CT):
                        pool.indirect_dma_start(rows[:, c, :], None, keep["xn_dram"],
                                                bass.IndirectOffsetOnAxis(rows_id[:, c:c + 1], 0)).then_inc(rows_in, 16)

                def adopt(n):
                    nc.gpsimd.tensor_copy(ids[:, :], next_ids[:, :]).then_inc(ids_ready, 1)
                    nc.gpsimd.tensor_copy(weight[:, :], rows_meta[:, :, bass.ds(n, 1)].rearrange("p c o -> p (c o)"))\
                        .then_inc(weight_ready, 1)
                    pool.wait_ge(weight_ready, n + 1)
                    alone(pool, passed)
                    for c in range(CT):
                        nc.gpsimd.tensor_tensor(bias_w[:, c, :], b2[:, bass.ds(n, 1), :].rearrange("p o d -> p (o d)"),
                                                weight[:, c:c + 1].to_broadcast([P, D]), ALU.mult).then_inc(bias_ready, 1)

                def add_rows(n):
                    pool.wait_ge(ids_ready, n + 1)
                    for c in range(CT):
                        pool.wait_ge(y_scaled, 1 + n * CT + c + 1)
                        alone(pool, passed)
                        pool.indirect_dma_start(io["out"], bass.IndirectOffsetOnAxis(ids[:, c:c + 1], 0), y[:, c, :],
                                                None, compute_op=ALU.add).then_inc(y_added, 16)

                fetch(0)
                pool.wait_ge(b2_loaded, 16)
                pool.wait_ge(keep["x_copied"], 16)
                with pool.Fori(0, E) as e:
                    adopt(e)
                    pool.wait_ge(weight_ready, e + 1)
                    pool.wait_ge(ids_ready, e + 1)
                    fetch(e + 1)
                    add_rows(e)
                    pool.wait_ge(y_added, (e + 1) * CT * 16)
                    alone(pool, passed)
                pool.wait_ge(rows_in, (E + 1) * CT * 16)

            @block.scalar
            def _(act):
                def split(turns, slot):
                    act.wait_ge(w_in[slot], (turns + 1) * 16)
                    nc.scalar.activation(w_hi[:, slot, :], w_raw[:, slot, :], ACT.Copy).then_inc(w_hi_ready, 1)

                def turned(n, k, side, b_x):
                    act.wait_ge(x_turned, n * KD + k + 1)
                    nc.scalar.activation(xT_hi[:, bass.ds(side, 1), k, :].rearrange("p o c -> p (o c)"), b_x[:, :],
                                         ACT.Copy).then_inc(x_hi_ready, 1)

                split(0, 0)
                split(0, 1)
                for k in range(KD):
                    turned(0, k, 0, b_y[k])
                act.wait_ge(b1_loaded, 16)
                nc.scalar.activation(warm[:, :], b1[:, 0, 0:1], ACT.Gelu).then_inc(passed, 1)
                with act.Fori(0, E) as e:
                    side = act.snap((e + 1) % 2)
                    for f in range(FT):
                        g = e * FT + f
                        act.wait_ge(h_ready, g + 1)
                        nc.scalar.activation(h[:, f % HB, :], b_h[f % 2][:, :], ACT.Gelu,
                                             bias=b1[:, bass.ds(e, 1), f].rearrange("p o -> p o")).then_inc(h_done, 1)
                        act.wait_ge(h_done, g + 1)
                        nc.scalar.activation(h_hi[:, f % HB, :], h[:, f % HB, :], ACT.Copy).then_inc(h_hi_ready, 1)
                        split(e * (FT // RING) + (f + 2) // RING, (f + 2) % RING)
                        if TURN <= f < TURN + KD:
                            turned(e + 1, f - TURN, side, b_x)

            @block.vector
            def _(dve):
                def split(g, slot):
                    dve.wait_ge(w_hi_ready, g + 1)
                    nc.vector.tensor_tensor(w_lo[:, slot, :], w_raw[:, slot, :], f32(w_hi[:, slot, :]), ALU.subtract)\
                        .then_inc(w_lo_ready, 1)

                def hot(n, part):
                    if part == 0:
                        dve.wait_ge(list_summed, n)
                        nc.vector.tensor_tensor(hot_a[:, :, :], keep["pos_a"][:, bass.ds(n, 1), :]
                                                .rearrange("p o t -> p (o t)").unsqueeze(2).to_broadcast([P, NT, 16]),
                                                keep["ids_a"][:, :].unsqueeze(1).to_broadcast([P, NT, 16]),
                                                ALU.is_equal).then_inc(f_hot, 1)
                    elif part == 1:
                        nc.vector.tensor_tensor(hot_b[:, :, :], keep["pos_b"][:, bass.ds(n, 1), :]
                                                .rearrange("p o t -> p (o t)").unsqueeze(2).to_broadcast([P, NT, 32]),
                                                keep["ids_b"][:, :].unsqueeze(1).to_broadcast([P, NT, 32]),
                                                ALU.is_equal).then_inc(f_hot, 1)
                    elif part == 2:
                        dve.wait_ge(f_hot, n * 3 + 2)
                        nc.vector.tensor_tensor(named[:, :, 0, :], hot_b[:, :, :],
                                                spread(keep["tile_ids"][:, :], [P, NT, 32]), ALU.mult).then_inc(f_hot, 1)
                    else:
                        dve.wait_ge(f_hot, n * 3 + 3)
                        nc.vector.tensor_scalar(named[:, :, 1, :], hot_b[:, :, :], keep["part_id"][:, :], None,
                                                ALU.mult).then_inc(hot_ready, 1)

                def name(n):
                    dve.wait_ge(list_summed, n + 1)
                    nc.vector.tensor_copy(name_f[:, :], b_list[0:16, 32:64]).then_inc(f_list, 1)
                    dve.wait_ge(f_list, n + 1)
                    dve.wait_ge(list_moved, n * 16)
                    nc.vector.scalar_tensor_tensor(list_i[:, :], b_list[0:16, 0:32], float(P), name_f[:, :],
                                                   ALU.mult, ALU.add).then_inc(list_ready, 1)

                def turned(n, k, side, b_x):
                    dve.wait_ge(x_hi_ready, n * KD + k + 1)
                    nc.vector.tensor_tensor(xT_lo[:, bass.ds(side, 1), k, :].rearrange("p o c -> p (o c)"), b_x[:, :],
                                            f32(xT_hi[:, bass.ds(side, 1), k, :]).rearrange("p o c -> p (o c)"),
                                            ALU.subtract).then_inc(x_lo_ready, 1)

                def scale_rows(n):
                    dve.wait_ge(bias_ready, (n + 1) * CT)
                    for c in range(CT):
                        dve.wait_ge(y_ready, n * CT + c + 1)
                        nc.vector.scalar_tensor_tensor(y[:, c, :], b_y[c][:, :], weight[:, c:c + 1], bias_w[:, c, :],
                                                       ALU.mult, ALU.add).then_inc(y_scaled, 1)

                dve.sem_inc(y_scaled, 1)
                for part in range(4):
                    hot(0, part)
                name(0)
                split(0, 0)
                split(1, 1)
                for k in range(KD):
                    turned(0, k, 0, b_y[k])
                with dve.Fori(0, E) as e:
                    side = dve.snap((e + 1) % 2)
                    for f in range(FT):
                        g = e * FT + f
                        dve.wait_ge(h_hi_ready, g + 1)
                        nc.vector.tensor_tensor(h_lo[:, f % HB, :], h[:, f % HB, :], f32(h_hi[:, f % HB, :]),
                                                ALU.subtract).then_inc(h_lo_ready, 1)
                        split(g + 2, (f + 2) % RING)
                        if HOT <= f < HOT + 4:
                            hot(e + 1, f - HOT)
                        if f == NAME:
                            name(e + 1)
                        if TURN <= f < TURN + KD:
                            turned(e + 1, f - TURN, side, b_x)
                    scale_rows(e)

            @block.tensor
            def _(pe):
                def make_list(n):
                    pe.wait_ge(hot_ready, n + 1)
                    for t in range(NT):
                        last = nc.tensor.matmul(b_list[0:16, 0:64], hot_a[:, t, :],
                                                named[:, t, :, :].rearrange("p a b -> p (a b)"),
                                                start=(t == 0), stop=(t == NT - 1))
                    last.then_inc(list_summed, 1)

                def turn(n, k, b_x):
                    if k == 0:
                        pe.wait_ge(rows_in, (n + 1) * CT * 16)
                    for c in range(CT):
                        last = nc.tensor.transpose(b_x[:, c * P:(c + 1) * P], rows[:, c, k * P:(k + 1) * P],
                                                   keep["ident"][:, :])
                    last.then_inc(x_turned, 1)

                def fc1(g, f, sides):
                    pe.wait_ge(w_lo_ready, g + 1)
                    for k in range(KD):
                        cols = slice(k * P, (k + 1) * P)
                        last = matmul3(nc, b_h[f % 2][:, :], (w_hi[:, f % RING, cols], w_lo[:, f % RING, cols]),
                                       sides[k], k == 0, k == KD - 1)
                    last.then_inc(h_ready, 1)

                def fc2(e, g, f):
                    pe.wait_ge(h_lo_ready, g + 1)
                    for c in range(CT):
                        if f == 0 and c == 0:
                            pe.wait_ge(y_scaled, 1 + e * CT)
                        cols = slice(c * P, (c + 1) * P)
                        last = matmul3(nc, b_y[c][:, :], (h_hi[:, f % HB, cols], h_lo[:, f % HB, cols]),
                                       (w_hi[:, f % RING, D:2 * D], w_lo[:, f % RING, D:2 * D]), f == 0, f == FT - 1)
                        if f == FT - 1:
                            last.then_inc(y_ready, 1)

                make_list(0)
                for k in range(KD):
                    turn(0, k, b_y[k])
                with pe.Fori(0, E) as e:
                    side = pe.snap(e % 2)
                    pe.wait_ge(x_lo_ready, (e + 1) * KD)
                    sides = [(xT_hi[:, bass.ds(side, 1), k, :].rearrange("p o c -> p (o c)"),
                              xT_lo[:, bass.ds(side, 1), k, :].rearrange("p o c -> p (o c)")) for k in range(KD)]
                    for f in range(FT):
                        g = e * FT + f
                        fc1(g, f, sides)
                        if f > 0:
                            fc2(e, g - 1, f - 1)
                        if f == LIST:
                            make_list(e + 1)
                        if TURN <= f < TURN + KD:
                            pe.wait_ge(x_lo_ready, (e + 1) * KD + f - TURN)
                            turn(e + 1, f - TURN, b_x)
                    fc2(e, e * FT + FT - 1, FT - 1)


def program(nc, io):
    ctx = ExitStack()
    with ctx:
        def sb(name, shape, dt=F32):
            return ctx.enter_context(nc.sbuf_tensor(name, shape, dt))

        keep = {
            "ident": sb("ident", [P, P]),
            "logits": sb("logits", [P, NT + 1, E]),
            "seen": sb("seen_tiles", [P, NT]),
            "pos_a": sb("pos_a", [P, EP, NT], BF16),
            "pos_b": sb("pos_b", [P, EP, NT], BF16),
            "ids_a": sb("ids_a", [P, 16], BF16), "ids_b": sb("ids_b", [P, 32], BF16),
            "tile_ids": sb("tile_ids", [P, NT], BF16), "part_id": sb("part_id", [P, 1]),
            "x_copied": ctx.enter_context(nc.semaphore("x_copied")),
            "xn_filled": ctx.enter_context(nc.semaphore("xn_filled")),
            "xn_dram": nc.dram_tensor("xn_dram", [(NT + 1) * P, D], F32).ap(),
            "meta_dram": nc.dram_tensor("meta_dram", [N, META], F32).ap(),
            "kl_dram": nc.dram_tensor("kl_dram", [NPAIR, KCOLS], I32).ap(),
        }
        with ExitStack() as scope:
            def sa(name, shape, dt=F32):
                return scope.enter_context(nc.sbuf_tensor(name, shape, dt))

            keep |= {
                "half": sa("half", [P, 1]),
                "causal": sa("causal", [P, 2, P]),
                "hidden": sa("hidden", [P, NT + 1, P], BF16),
                "has_key": sa("has_key", [P, NT]),
                "kl": sa("kl_row", [1, NPAIR * KCOLS], I32),
                "wq_hi": sa("wq_hi", [P, KD, H * DH], F32R), "wq_lo": sa("wq_lo", [P, KD, H * DH], F32R),
                "wkv_hi": sa("wkv_hi", [P, KD, 3 * DH], F32R), "wkv_lo": sa("wkv_lo", [P, KD, 3 * DH], F32R),
                "wo_hi": sa("wo_hi", [P, KO, D], F32R), "wo_lo": sa("wo_lo", [P, KO, D], F32R),
                "v_hi": sa("v_hi", [P, VW], F32R), "v_lo": sa("v_lo", [P, VW], F32R),
                "null_k": sa("null_k_row", [P, DH]), "null_v": sa("null_v_row", [P, VW]), "null_bias": sa("null_bias_row", [P, H]),
                "g_in": sa("g_in_row", [P, D]), "g_out": sa("g_out_row", [P, D]), "norm_w": sa("norm_w_row", [P, D]),
                "router_b": sa("router_b_row", [P, E]), "router_wT": sa("router_wT_sb", [P, KD, E]),
            }
            make_lists(nc, ctx, io, keep)
            attend(nc, ctx, io, keep)
        route(nc, ctx, io, keep)
        experts(nc, ctx, io, keep)


def kernel(x, fside_16xSxS_0, cond_64, mask_BxS_bk0, L0_cond_g_in, L0_cond_null_attn_bias, L0_cond_Wq,
           L0_cond_Wkv, L0_cond_Wo, L0_cond_g_out, L0_ffn_norm_weight, L0_ffn_router_weight,
           L0_ffn_router_bias, L0_ffn_fc1_weight, L0_ffn_fc1_bias, L0_ffn_fc2_weight, L0_ffn_fc2_bias):
    import numpy as np

    import concourse.bacc as bacc
    from concourse.bass_utils import run_bass_kernel_spmd

    a = np.asarray
    wkv = a(L0_cond_Wkv)
    wk, wv = wkv[:, :DH], wkv[:, DH:]
    cond = a(cond_64)
    w1 = a(L0_ffn_fc1_weight).reshape(E, FT, P, KD, P).transpose(0, 1, 4, 3, 2).reshape(E, FT, P, D)
    w2 = a(L0_ffn_fc2_weight).reshape(E, D, FT, P).transpose(0, 2, 3, 1)
    arrays = {
        "x": a(x).reshape(N, D),
        "bias": a(fside_16xSxS_0).reshape(H, QT, P, QT, P).transpose(1, 3, 2, 0, 4).reshape(QT * QT * P, H * P),
        "mask": a(mask_BxS_bk0).reshape(1, N),
        "wq": a(L0_cond_Wq).reshape(KD, P, H * DH).transpose(1, 0, 2),
        "wkv": np.concatenate([wk, wk, wv], 1).reshape(KD, P, 3 * DH).transpose(1, 0, 2),
        "wo": a(L0_cond_Wo).reshape(H, DH, D).reshape(KO, P, D).transpose(1, 0, 2),
        "null_k": cond[0:1],
        "null_v": np.concatenate([cond[1], np.ones(1, np.float32), np.zeros(1, np.float32)]).reshape(1, VW),
        "null_bias": a(L0_cond_null_attn_bias).reshape(1, H),
        "g_in": a(L0_cond_g_in).reshape(1, D), "g_out": a(L0_cond_g_out).reshape(1, D),
        "norm_w": a(L0_ffn_norm_weight).reshape(1, D),
        "router_wT": a(L0_ffn_router_weight).reshape(E, KD, P).transpose(2, 1, 0),
        "router_b": a(L0_ffn_router_bias).reshape(1, E),
        "w": np.concatenate([w1, w2], 3).reshape(E * FT, P, 2 * D),
        "b1": a(L0_ffn_fc1_bias).reshape(E, FT, P).transpose(2, 0, 1),
        "b2": a(L0_ffn_fc2_bias).reshape(1, E * D),
    }
    arrays = {name: np.ascontiguousarray(v) for name, v in arrays.items()}
    nc = bacc.Bacc("TRN2", target_bir_lowering=False, num_devices=1)
    io = {name: nc.dram_tensor("in_" + name, v.shape, mybir.dt.from_np(v.dtype), kind="ExternalInput").ap()
          for name, v in arrays.items()}
    io["out"] = nc.dram_tensor("out", (N, D), F32, kind="ExternalOutput").ap()
    program(nc, io)
    got = run_bass_kernel_spmd(nc, [{"in_" + name: v for name, v in arrays.items()}], core_ids=[0])
    return got.results[0]["out"].reshape(B, S, D)
```
